# Optimizing a Trainium2 kernel written in Bass

```python
import numpy as np
import jax
import jax.numpy as jnp

def _softmax(x, axis=-1):
    return jax.nn.softmax(x, axis=axis)

def _gelu(x):
    return jax.nn.gelu(x, approximate=True)

def _silu(x):
    return jax.nn.silu(x)

def _sigmoid(x):
    return jax.nn.sigmoid(x)

def _layernorm(x, axis=-1, eps=1e-05):
    m = jnp.mean(x, axis=axis, keepdims=True)
    v = jnp.var(x, axis=axis, keepdims=True)
    return (x - m) / jnp.sqrt(v + eps)

def _scatter_add(tgt, idx, src, axis=0):
    return tgt.at[idx].add(src)

def _segment_sum(src, seg, n):
    return jax.ops.segment_sum(src, seg, n)
kernel_name = 'mk_prb_d1_jaxref_r8_197b30'

def setup_inputs(seed: int=0):
    np.random.seed(seed)
    _w = jnp.asarray

    def _L0_attn_setup():
        import jax, jax.numpy as jnp
        import numpy as np
        import math
        HIDDEN = 128
        HEADS = 16
        HEAD_DIM = HIDDEN // HEADS
        key = jax.random.key(seed)
        ks = jax.random.split(key, 7)
        B, S = (2, 256)
        scale = 1.0 / math.sqrt(HIDDEN)
        return {'x': jax.random.normal(ks[0], (B, S, HIDDEN), dtype=jnp.float32), 'Wq': jax.random.normal(ks[1], (HIDDEN, HIDDEN), dtype=jnp.float32) * scale, 'Wk': jax.random.normal(ks[2], (HIDDEN, HIDDEN), dtype=jnp.float32) * scale, 'Wv': jax.random.normal(ks[3], (HIDDEN, HIDDEN), dtype=jnp.float32) * scale, 'Wo': jax.random.normal(ks[4], (HIDDEN, HIDDEN), dtype=jnp.float32) * scale, 'quantum_phase': jax.random.normal(ks[5], (HEADS, HEAD_DIM), dtype=jnp.float32), 'quantum_amplitude': jnp.ones((HEADS, HEAD_DIM), dtype=jnp.float32)}
    _L0_attn_in = _L0_attn_setup()

    def _L0_ffn_setup():
        import jax, jax.numpy as jnp
        import numpy as np
        TOP_K = 2
        key = jax.random.key(seed)
        k1, k2, k3, k4 = jax.random.split(key, 4)
        B, S, H, F, E = (2, 256, 128, 352, 8)
        hidden_states = jax.random.normal(k1, (B, S, H), dtype=jnp.float32)
        wqkv = jax.random.normal(k2, (3 * E, H), dtype=jnp.float32) * 0.02
        w1 = jax.random.normal(k3, (E, 2 * F, H), dtype=jnp.float32) * 0.02
        w2 = jax.random.normal(k4, (E, H, F), dtype=jnp.float32) * 0.02
        return {'hidden_states': hidden_states, 'wqkv': wqkv, 'w1': w1, 'w2': w2}
    _L0_ffn_in = _L0_ffn_setup()
    _d = {'L0_attn_x': _L0_attn_in['x'], 'L0_attn_Wq': _L0_attn_in['Wq'], 'L0_attn_Wk': _L0_attn_in['Wk'], 'L0_attn_Wv': _L0_attn_in['Wv'], 'L0_attn_Wo': _L0_attn_in['Wo'], 'L0_attn_quantum_phase': _L0_attn_in['quantum_phase'], 'L0_attn_quantum_amplitude': _L0_attn_in['quantum_amplitude'], 'L0_ffn_wqkv': _L0_ffn_in['wqkv'], 'L0_ffn_w1': _L0_ffn_in['w1'], 'L0_ffn_w2': _L0_ffn_in['w2']}
    _x0 = _d['L0_attn_x']
    _d['L0_attn_x'] = jax.random.normal(jax.random.fold_in(jax.random.key(seed), 1), (1, 2048, 128), dtype=_x0.dtype)
    del _x0
    return _d

def reference(L0_attn_x, L0_attn_Wq, L0_attn_Wk, L0_attn_Wv, L0_attn_Wo, L0_attn_quantum_phase, L0_attn_quantum_amplitude, L0_ffn_wqkv, L0_ffn_w1, L0_ffn_w2):

    def _L0_attn_ref(x, Wq, Wk, Wv, Wo, quantum_phase, quantum_amplitude):
        import jax, jax.numpy as jnp
        import numpy as np
        import math
        HIDDEN = 128
        HEADS = 16
        HEAD_DIM = HIDDEN // HEADS
        B, S, d = x.shape
        H, D = (HEADS, HEAD_DIM)
        mod = (jnp.cos(quantum_phase) * quantum_amplitude)[None, :, None, :]

        def proj(W):
            return (x @ W).reshape(B, S, H, D).transpose(0, 2, 1, 3)
        q = proj(Wq) * mod
        k = proj(Wk) * mod
        v = proj(Wv) * mod
        scores = jnp.einsum('bhid,bhjd->bhij', q, k) / math.sqrt(D)
        idx = jnp.arange(S, dtype=jnp.float32)
        cos_mat = jnp.cos(2.0 * math.pi * (idx[:, None] - idx[None, :]) / S)
        scores = scores * cos_mat
        w = jax.nn.softmax(scores, axis=-1)
        w = (w + jnp.roll(w, 1, axis=-1)) / math.sqrt(2.0)
        out = jnp.einsum('bhij,bhjd->bhid', w, v)
        out = out.transpose(0, 2, 1, 3).reshape(B, S, d)
        return out @ Wo

    def _L0_ffn_ref(hidden_states, wqkv, w1, w2):
        import jax, jax.numpy as jnp
        import numpy as np
        TOP_K = 2
        b, s, h = hidden_states.shape
        E = w1.shape[0]
        mixed = hidden_states @ wqkv.T
        q, k, v = jnp.split(mixed, 3, axis=-1)
        q = q.astype(jnp.float32)
        k = k.astype(jnp.float32)
        v = v.astype(jnp.float32)
        attn = jax.nn.softmax(q[..., :, None] * k[..., None, :], axis=-1)
        logits = jnp.einsum('bsej,bsj->bse', attn, v).reshape(-1, E)
        top_logits, idx = jax.lax.top_k(logits, TOP_K)
        scores = jax.nn.softmax(top_logits.astype(jnp.float32), axis=-1).astype(hidden_states.dtype)
        N = b * s
        x = hidden_states.reshape(N, h)
        token_ids = jnp.repeat(jnp.arange(N), TOP_K)
        expert_ids = idx.reshape(-1)
        x_rep = x[token_ids]
        out = jnp.zeros_like(x_rep)
        for e in range(E):
            h1 = x_rep @ w1[e].T
            a, g = jnp.split(h1, 2, axis=-1)
            he = jax.nn.silu(a) * g @ w2[e].T
            out = out + jnp.where((expert_ids == e)[:, None], he, jnp.zeros((), out.dtype))
        out = out * scores.reshape(-1, 1)
        combined = out.reshape(N, TOP_K, h).sum(axis=1)
        return combined.reshape(b, s, h)
    x = L0_attn_x
    xn = _layernorm(x, axis=-1)
    x = x + _L0_attn_ref(xn, L0_attn_Wq, L0_attn_Wk, L0_attn_Wv, L0_attn_Wo, L0_attn_quantum_phase, L0_attn_quantum_amplitude) + _L0_ffn_ref(xn, L0_ffn_wqkv, L0_ffn_w1, L0_ffn_w2)
    return x

_drawn_inputs = setup_inputs


def setup_inputs(seed=0):
    import zlib

    import numpy as np

    out = dict(_drawn_inputs(seed))
    spreads = {'L0_attn_quantum_amplitude': (1.0, 0.6)}
    factors = {'L0_attn_Wq': 3.564,
     'L0_attn_Wk': 3.18,
     'L0_attn_quantum_phase': 3.175,
     'L0_ffn_wqkv': 8.0,
     'L0_ffn_w1': 8.0,
     'L0_ffn_w2': 8.0}
    for name, (base, spread) in spreads.items():
        noise = np.random.default_rng([zlib.crc32(name.encode()), seed]).standard_normal(out[name].shape)
        drawn = base * np.exp(spread * noise) if base else spread * noise
        out[name] = jnp.asarray(drawn.astype(out[name].dtype))
    for name, factor in factors.items():
        out[name] = (out[name] * factor).astype(out[name].dtype)
    return out
```

```python
from contextlib import ExitStack

import numpy as np

import concourse.bass as bass
from concourse import mybir

F32 = mybir.dt.float32
BF16 = mybir.dt.bfloat16
ALU = mybir.AluOpType
ACT = mybir.ActivationFunctionType
AX = mybir.AxisListType.X

P = 128
S = 2048
DM = 128
H = 16
D = 8
E = 8
F = 352
NT = S // P
CW = 512
NC = S // CW
FCH = [(0, 128), (128, 128), (256, 96)]
NF = len(FCH)
ROWS = 2 * D
KQ = 6 * ROWS
KS = KQ + 2
STEPS = NT
CREDIT = 2
TURNED = 1
ADDED = NC
ISQ8 = float(1.0 / np.sqrt(D))
TWO_PI = 2.0 * np.pi
PI_A = 6.28125
PI_B = float(np.float32(2.0 ** -20 * np.floor((TWO_PI - PI_A) * 2.0 ** 20)))
PI_C = float(TWO_PI - PI_A - PI_B)
ROUND = 12582912.0
PI_DOWN = 3.1415925
LOWEST = -3.0e38
EPS = 1e-5
SCORE_BANKS, O_BANK, T_BANK, M_BANK = 0, 4, 5, 6
LEAD = 12


def build(nc, x, Wq, Wk, Wv, Wo, phase, amp, wqkv, w1, w2, ident_in, desc_in, cs_in, out):
    scratch = nc.dram_tensor("qk_parts", [2, 3, H, ROWS, S], BF16, kind="Internal").ap()
    x_v = x.rearrange("a (t p) d -> p (a t) d", p=P)
    out_v = out.rearrange("a (t p) d -> p (a t) d", p=P)

    with ExitStack() as ctx:
        def sb(name, shape, dt):
            return ctx.enter_context(nc.sbuf_tensor(name, shape, dt))

        def sem(name):
            return ctx.enter_context(nc.semaphore(name))

        acc = sb("acc", [P, NT, DM], F32)
        xnT = sb("xnT", [P, S + 1], F32)
        big = sb("big", [P, 4, S], F32)
        rotated = [big[:, i, :] for i in range(4)]
        xn = big[:, 3, :].rearrange("p (t d) -> p t d", d=DM)
        probs = big[:, 0:2, :].rearrange("p a (b c n) -> p a b c n", b=2, c=2)
        attn = big[:, 2, :].rearrange("p (t d) -> p t d", d=DM)
        parts = sb("parts", [P, 4, 3, S], BF16)
        cs = sb("cs", [P, S], F32)
        ident = sb("ident", [P, P], F32)
        desc = sb("desc", [P, E], F32)
        wmat = sb("wmat", [P, 4, DM], F32)
        wo_mod = sb("wo_mod", [P, DM], F32)
        wqkv_sb = sb("wqkv_sb", [3 * E, DM], F32)
        wqkvT = sb("wqkvT", [P, 3 * E], F32)
        stats = sb("stats", [P, NT, 6], F32)
        mv = sb("mv", [P, NT, 2], F32)
        ve = sb("ve", [P, 4, NT], F32)
        rstd = sb("rstd", [P, NT], F32)
        ang = sb("ang", [P, 8, 3], F32)
        mod = sb("mod", [P, 3], F32)
        mix = sb("mix", [P, NT, 3 * E], F32)
        pair = sb("pair", [P, NT, E, E], F32)
        gate = sb("gate", [P, 8, NT, E], F32)
        top = sb("top", [P, 8, NT], F32)
        pw = sb("pw", [P, E, NT], F32)
        w1raw = sb("w1raw", [P, 2, 2 * NF, DM], F32)
        w2raw = sb("w2raw", [P, 2, F], F32)
        w1T = sb("w1T", [P, 2, 2 * F], F32)
        w2T = sb("w2T", [P, 2, NF, DM], F32)
        silu = sb("silu", [P, 2, CW], F32)
        hid = sb("hid", [P, 2, NF, CW], F32)
        vaug = sb("vaug", [P, H, NT, D + 1], F32)
        vh = sb("vh", [P, 2, NT, 32], F32)
        qa = [sb(f"qa{i}", [KS, S], BF16) for i in range(2)]
        ka = [sb(f"ka{i}", [KS, S], BF16) for i in range(2)]
        m4 = sb("m4", [P, NT, NC], F32)
        mx = sb("mx", [P, 2, 8], F32)
        shift = sb("shift", [8, 2, P], BF16)
        osb = sb("osb", [P, CW], F32)
        half_sum = sb("half_sum", [P, 4, 2, D + 1], F32)
        sums = sb("sums", [P, 4, 2, D + 1], F32)
        rden = sb("rden", [P, 4, 2, 1], F32)
        attnT = sb("attnT", [P, S], F32)
        ps = ctx.enter_context(nc.psum_tensor("ps", [P, 8, CW], F32))

        x_in = [sem(f"x_in{i}") for i in range(4)]
        ident_ld, const_ld, wmat_ld, phase_ld, cs_ld = (sem(n) for n in ("ident_ld", "const_ld", "wmat_ld", "phase_ld", "cs_ld"))
        w_ld = [sem(f"w_ld{i}") for i in range(2)]
        dve_step, var_ready, sd_ready, xn_ready = (sem(n) for n in ("dve_step", "var_ready", "sd_ready", "xn_ready"))
        xt_ps, xt_ready, wrap_ready = (sem(n) for n in ("xt_ps", "xt_ready", "wrap_ready"))
        ang_ready, sin_ready, mod_ready = (sem(n) for n in ("ang_ready", "sin_ready", "mod_ready"))
        wqkv_ps, wqkv_ready, mix_ps, mix_ready = (sem(n) for n in ("wqkv_ps", "wqkv_ready", "mix_ps", "mix_ready"))
        gexp_in, gexp_out, pw_ready = (sem(n) for n in ("gexp_in", "gexp_out", "pw_ready"))
        proj_ps, rot_ready, v_ps, v_ready, ones_ready = (sem(n) for n in ("proj_ps", "rot_ready", "v_ps", "v_ready", "ones_ready"))
        split_step, parts_ready, scratch_wr = (sem(n) for n in ("split_step", "parts_ready", "scratch_wr"))
        tr_ready, wT_ready = sem("tr_ready"), sem("wT_ready")
        a_ready, g_ready, silu_ready, hid_ready, y_ready, y_added = (
            sem(n) for n in ("a_ready", "g_ready", "silu_ready", "hid_ready", "y_ready", "y_added"))
        aug_ld, score_ready, exp_done, pv_done, vh_ready = (
            sem(n) for n in ("aug_ld", "score_ready", "exp_done", "pv_done", "vh_ready"))
        m_ready, m_reduced, mx_ready, mxT_ready, shift_hi, shift_ready, shift_ld = (
            sem(n) for n in ("m_ready", "m_reduced", "mx_ready", "mxT_ready", "shift_hi", "shift_ready", "shift_ld"))
        o_copied, ot_ready, half_ready, sum_ready, rden_ready, attn_ready = (
            sem(n) for n in ("o_copied", "ot_ready", "half_ready", "sum_ready", "rden_ready", "attn_ready"))
        at_ps, at_ready, fin_ps, fin_ready, out_wr, wo_ready = (
            sem(n) for n in ("at_ps", "at_ready", "fin_ps", "fin_ready", "out_wr", "wo_ready"))

        block = ctx.enter_context(nc.Block())

        def head_steps():
            first = [(0, s) for s in range(3)]

            def body(h0, last):
                steps = [(h0, 0, s) for s in range(3, STEPS)] + [(h0 + 1, 1, s) for s in range(STEPS)]
                return steps if last else steps + [(h0 + 2, 0, s) for s in range(3)]
            return [(h, 0, s) for h, s in first], body

        first_steps, pair_steps = head_steps()

        def run_steps(eng, step):
            for h, par, s in first_steps:
                step(h, par, s, True, False)
            with eng.Fori(0, H // 2 - 1) as pr:
                for h, par, s in pair_steps(pr * 2, False):
                    step(h, par, s, False, False)
            for h, par, s in pair_steps(H - 2, True):
                step(h, par, s, False, h == H - 1)

        @block.sync
        def _(sp):
            for i in range(4):
                sp.dma_start(acc[:, 4 * i:4 * i + 4, :], x_v[:, 4 * i:4 * i + 4, :]).then_inc(x_in[i], 16)
            sp.dma_start(ident[:], ident_in).then_inc(ident_ld, 16)
            sp.dma_start(desc[:], desc_in).then_inc(const_ld, 16)
            sp.dma_start(wqkv_sb[:], wqkv).then_inc(const_ld, 16)
            for i, w in enumerate((Wq, Wk, Wv, Wo)):
                sp.dma_start(wmat[:, i, :], w).then_inc(wmat_ld, 16)
            for src, at in ((phase, 0), (amp, 1)):
                for g in range(2):
                    for half in range(2):
                        sp.dma_start(ang[64 * half:64 * half + 64, at, g:g + 1],
                                     src[8 * g:8 * g + 8, :].rearrange("h (d o) -> (h d) o", o=1)).then_inc(phase_ld, 16)
                sp.dma_start(ang[:, at, 2:3], src.rearrange("h (d o) -> (h d) o", o=1)).then_inc(phase_ld, 16)

            def load_expert(e, par):
                for b in range(2):
                    sp.dma_start(w1raw[:, par, NF * b:NF * b + 2, :],
                                 w1[e, F * b:F * b + 256, :].rearrange("(c p) h -> p c h", p=P)).then_inc(w_ld[par], 16)
                    sp.dma_start(w1raw[0:96, par, NF * b + 2, :], w1[e, F * b + 256:F * b + F, :]).then_inc(w_ld[par], 16)
                sp.dma_start(w2raw[:, par, :], w2[e]).then_inc(w_ld[par], 16)

            load_expert(0, 0)
            load_expert(1, 1)
            sp.dma_start(cs[:], cs_in).then_inc(cs_ld, 16)
            with sp.Fori(0, E // 2 - 1) as pr:
                for par in range(2):
                    e = pr * 2 + par
                    sp.wait_ge(tr_ready, e * NF + NF)
                    load_expert(e + 2, par)

            for i in range(4):
                sp.wait_ge(parts_ready, i + 1)
                g, which = i // 2, i % 2
                for part in range(3):
                    for half in range(2):
                        sp.dma_start(scratch[which, part, 8 * g:8 * g + 8, 8 * half:8 * half + 8, :],
                                     parts[64 * half:64 * half + 64, i, part, :]).then_inc(scratch_wr, 16)
            sp.wait_ge(scratch_wr, 24 * 16)

            def load_head(h, par):
                q_parts, k_parts = (0, 0, 0, 1, 1, 2), (0, 1, 2, 0, 1, 0)
                for buf, which, order in ((qa[par], 0, q_parts), (ka[par], 1, k_parts)):
                    for b, part in enumerate(order):
                        sp.dma_start(buf[ROWS * b:ROWS * b + ROWS, :], scratch[which, part, h, :, :]).then_inc(aug_ld, 16)

            def load_shift(h, par, half):
                sp.wait_ge(shift_ready, h * 2 + half + 1)
                for r in range(2):
                    sp.dma_start(qa[par][KQ + r:KQ + r + 1, 1024 * half:1024 * half + 1024].rearrange("o (t p) -> o t p", p=P),
                                 shift[:, r, :]).then_inc(shift_ld, 16)

            load_head(0, 0)
            load_shift(0, 0, 0)

            def step(h, par, s, first, last):
                if s == 0 and not last:
                    sp.wait_ge(score_ready, h * (2 * STEPS))
                    load_head(h + 1, 1 - par)
                if s == 5:
                    load_shift(h, par, 1)
                if s == 13 and not last:
                    load_shift(h + 1, 1 - par, 0)

            run_steps(sp, step)
            for q in range(4):
                sp.wait_ge(fin_ready, q + 1)
                sp.dma_start(out_v[:, 4 * q:4 * q + 4, :], acc[:, 4 * q:4 * q + 4, :]).then_inc(out_wr, 16)
            sp.wait_ge(out_wr, 4 * 16)

        @block.gpsimd
        def _(pool):
            nc.gpsimd.memset(vaug[:], 1.0).then_inc(ones_ready, 1)
            nc.gpsimd.memset(vh[:], 0.0).then_inc(ones_ready, 1)
            done = 0
            for i in range(4):
                pool.wait_ge(rot_ready, 4 * (i + 1))
                for part in range(3):
                    nc.gpsimd.tensor_copy(parts[:, i, part, :], rotated[i]).then_inc(split_step if part < 2 else parts_ready, 1)
                    if part < 2:
                        done += 1
                        pool.wait_ge(split_step, done)
                        nc.gpsimd.tensor_tensor(rotated[i], rotated[i], parts[:, i, part, :], ALU.subtract).then_inc(split_step, 1)
                        done += 1
                        pool.wait_ge(split_step, done)

            def head_values(h, par):
                nc.gpsimd.tensor_copy(vh[:, par, :, 0:D + 1], vaug[:, bass.ds(h, 1), :, :].rearrange("p o t d -> p (o t) d")).then_inc(vh_ready, 1)

            pool.wait_ge(v_ready, 4)
            pool.wait_ge(ones_ready, 4)
            head_values(0, 0)

            def step(h, par, s, first, last):
                if s == 1 and not last:
                    pool.wait_ge(pv_done, h * STEPS + CREDIT)
                    head_values(h + 1, 1 - par)

            run_steps(pool, step)

        @block.scalar
        def _(act):
            act.sem_inc(wT_ready, CREDIT)
            act.sem_inc(silu_ready, CREDIT)
            act.sem_inc(exp_done, CREDIT)
            act.wait_ge(var_ready, 1)
            nc.scalar.activation(ve[:, 1, :], ve[:, 0, :], ACT.Sqrt).then_inc(sd_ready, 1)
            act.wait_ge(ang_ready, 1)
            nc.scalar.activation(ang[:, 5, :], ang[:, 4, :], ACT.Sin, scale=0.5).then_inc(sin_ready, 1)
            act.wait_ge(wqkv_ps, 1)
            nc.scalar.copy(wqkvT[:], ps[:, 2, 0:3 * E]).then_inc(wqkv_ready, 1)
            for c in range(NC):
                act.wait_ge(xt_ps, c + 1)
                nc.scalar.copy(xnT[:, CW * c:CW * c + CW], ps[:, c % 2, :]).then_inc(xt_ready, 1)
            act.wait_ge(xt_ready, 1)
            nc.scalar.copy(xnT[:, S:S + 1], xnT[:, 0:1]).then_inc(wrap_ready, 1)
            act.wait_ge(ones_ready, 4)
            for q in range(4):
                act.wait_ge(v_ps, q + 1)
                nc.scalar.copy(vaug[:, :, 4 * q:4 * q + 4, 0:D],
                               ps[:, 6 + q % 2, :].rearrange("p (t h d) -> p h t d", t=4, h=H)).then_inc(v_ready, 1)

            def expert_weights(e, par):
                for b in range(NF):
                    act.wait_ge(tr_ready, e * NF + b + 1)
                    bank = 6 + (NF * par + b) % 2
                    if b < 2:
                        nc.scalar.copy(w1T[:, par, F * b:F * b + F], ps[:, bank, 0:F]).then_inc(wT_ready, 1)
                    else:
                        nc.scalar.copy(w2T[:, par, 0:2, :], ps[:, bank, 0:2 * DM].rearrange("p (c h) -> p c h", h=DM))
                        nc.scalar.copy(w2T[0:96, par, 2, :], ps[0:96, bank, 2 * DM:3 * DM]).then_inc(wT_ready, 1)

            expert_weights(0, 0)
            for r in range(2):
                act.wait_ge(gexp_in, r + 1)
                if r == 0:
                    nc.scalar.activation(pair[:], pair[:], ACT.Exp).then_inc(gexp_out, 1)
                else:
                    nc.scalar.activation(top[:, 5, :], top[:, 4, :], ACT.Exp).then_inc(gexp_out, 1)

            def expert(e, par, last):
                for k in range(NC * NF):
                    f = k % NF
                    n = e * (NC * NF) + k
                    rows = FCH[f][1]
                    act.wait_ge(a_ready, n + 1)
                    act.wait_ge(hid_ready, n - 1 + CREDIT)
                    nc.scalar.activation(silu[0:rows, k % 2, :], ps[0:rows, k % 2, :], ACT.Silu).then_inc(silu_ready, 1)
                if not last:
                    expert_weights(e + 1, 1 - par)

            with act.Fori(0, E // 2 - 1) as pr:
                for par in range(2):
                    expert(pr * 2 + par, par, False)
            expert(E - 2, 0, False)
            expert(E - 1, 1, True)

            def copy_out(unit, steps_done):
                act.wait_ge(pv_done, steps_done + CREDIT)
                act.wait_ge(ot_ready, unit + TURNED)
                nc.scalar.copy(osb[:], ps[:, O_BANK, :]).then_inc(o_copied, 1)

            def step(h, par, s, first, last):
                g = h * STEPS + s
                for b in range(2):
                    act.wait_ge(score_ready, g * 2 + b + 1)
                    act.wait_ge(pv_done, g - 1 + CREDIT)
                    nc.scalar.activation(probs[:, s % 2, b, :, :], ps[:, 2 * b:2 * b + 2, :], ACT.Exp, scale=ISQ8).then_inc(exp_done, 1)
                if s == 0 and not first:
                    copy_out(h * 2 - 1, g)
                if s == 8:
                    copy_out(h * 2, g)

            run_steps(act, step)
            copy_out(2 * H - 1, H * STEPS)
            for q in range(4):
                act.wait_ge(at_ps, q + 1)
                nc.scalar.copy(attnT[:, CW * q:CW * q + CW], ps[:, q, :]).then_inc(at_ready, 1)

        @block.vector
        def _(dve):
            chain = [0]

            def then(ins):
                chain[0] += 1
                ins.then_inc(dve_step, 1)
                dve.wait_ge(dve_step, chain[0])

            dve.sem_inc(m_reduced, CREDIT)
            dve.sem_inc(sum_ready, TURNED)
            dve.sem_inc(attn_ready, TURNED)
            dve.sem_inc(hid_ready, CREDIT)
            dve.sem_inc(y_added, ADDED)
            for i in range(2):
                nc.vector.memset(ka[i][KQ:KS, :], 1.0).then_inc(ones_ready, 1)
            for t in range(NT):
                if t % 4 == 0:
                    dve.wait_ge(x_in[t // 4], 16)
                ins = nc.vector.bn_stats(stats[:, t, :], acc[:, t, :])
            then(ins)
            for t in range(NT):
                ins = nc.vector.bn_aggr(mv[:, t, :], stats[:, t, :])
            then(ins)
            nc.vector.tensor_scalar(ve[:, 0, :], mv[:, :, 1], EPS, None, ALU.add).then_inc(var_ready, 1)
            dve.wait_ge(sd_ready, 1)
            then(nc.vector.reciprocal(rstd[:], ve[:, 1, :]))
            then(nc.vector.tensor_tensor(ve[:, 2, :], rstd[:], rstd[:], ALU.mult))
            then(nc.vector.tensor_tensor(ve[:, 3, :], ve[:, 2, :], ve[:, 0, :], ALU.mult))
            then(nc.vector.tensor_scalar(ve[:, 2, :], ve[:, 3, :], -0.5, 1.5, ALU.mult, ALU.add))
            then(nc.vector.tensor_tensor(rstd[:], rstd[:], ve[:, 2, :], ALU.mult))
            for t in range(NT):
                nc.vector.tensor_scalar(xn[:, t, :], acc[:, t, :], mv[:, t, 0:1], rstd[:, t:t + 1],
                                        ALU.subtract, ALU.mult).then_inc(xn_ready, 1)
            dve.wait_ge(phase_ld, 10 * 16)
            then(nc.vector.tensor_scalar(ang[:, 2, :], ang[:, 0, :], float(1.0 / TWO_PI), ROUND, ALU.mult, ALU.add))
            then(nc.vector.tensor_scalar(ang[:, 3, :], ang[:, 2, :], ROUND, None, ALU.subtract))
            then(nc.vector.scalar_tensor_tensor(ang[:, 4, :], ang[:, 3, :], -PI_A, ang[:, 0, :], ALU.mult, ALU.add))
            then(nc.vector.scalar_tensor_tensor(ang[:, 6, :], ang[:, 3, :], -PI_B, ang[:, 4, :], ALU.mult, ALU.add))
            then(nc.vector.scalar_tensor_tensor(ang[:, 7, :], ang[:, 3, :], -PI_C, ang[:, 6, :], ALU.mult, ALU.add))
            nc.vector.tensor_scalar(ang[:, 4, :], ang[:, 7, :], PI_DOWN, -PI_DOWN, ALU.min, ALU.max).then_inc(ang_ready, 1)
            dve.wait_ge(sin_ready, 1)
            then(nc.vector.tensor_tensor(ang[:, 6, :], ang[:, 5, :], ang[:, 5, :], ALU.mult))
            then(nc.vector.tensor_scalar(ang[:, 7, :], ang[:, 6, :], -2.0, 1.0, ALU.mult, ALU.add))
            then(nc.vector.tensor_tensor(mod[:], ang[:, 7, :], ang[:, 1, :], ALU.mult))
            dve.wait_ge(wmat_ld, 4 * 16)
            nc.vector.tensor_scalar(wo_mod[:], wmat[:, 3, :], mod[:, 2:3], float(1.0 / np.sqrt(2.0)), ALU.mult, ALU.mult).then_inc(wo_ready, 1)

            def over_j(ap):
                return ap.unsqueeze(3).to_broadcast([P, NT, E, E])

            def over_e(ap):
                return ap.unsqueeze(2).to_broadcast([P, NT, E, E])

            def by_token(ap):
                return ap.unsqueeze(2).to_broadcast([P, NT, E])

            dve.wait_ge(mix_ps, 1)
            then(nc.vector.tensor_copy(mix[:], ps[:, 3, 0:NT * 3 * E].rearrange("p (t n) -> p t n", t=NT)))
            then(nc.vector.tensor_tensor(pair[:], over_j(mix[:, :, 0:E]), over_e(mix[:, :, E:2 * E]), ALU.mult))
            then(nc.vector.tensor_reduce(gate[:, 0, :, :], pair[:], AX, ALU.max))
            nc.vector.tensor_tensor(pair[:], pair[:], over_j(gate[:, 0, :, :]), ALU.subtract).then_inc(gexp_in, 1)
            dve.wait_ge(gexp_out, 1)
            then(nc.vector.tensor_reduce(gate[:, 1, :, :], pair[:], AX, ALU.add))
            then(nc.vector.tensor_tensor(pair[:], pair[:], over_e(mix[:, :, 2 * E:3 * E]), ALU.mult))
            then(nc.vector.tensor_reduce(gate[:, 2, :, :], pair[:], AX, ALU.add))
            then(nc.vector.reciprocal(gate[:, 3, :, :], gate[:, 1, :, :]))
            then(nc.vector.tensor_tensor(gate[:, 4, :, :], gate[:, 2, :, :], gate[:, 3, :, :], ALU.mult))
            dve.wait_ge(const_ld, 2 * 16)
            order = desc[:].unsqueeze(1).to_broadcast([P, NT, E])
            for r, (logits, mask) in enumerate(((4, 5), (6, 7))):
                then(nc.vector.tensor_reduce(top[:, r, :], gate[:, logits, :, :], AX, ALU.max))
                then(nc.vector.tensor_tensor(gate[:, 0, :, :], gate[:, logits, :, :], by_token(top[:, r, :]), ALU.is_equal))
                then(nc.vector.tensor_tensor(gate[:, 1, :, :], gate[:, 0, :, :], order, ALU.mult))
                then(nc.vector.tensor_reduce(top[:, 2 + r, :], gate[:, 1, :, :], AX, ALU.max))
                then(nc.vector.tensor_tensor(gate[:, mask, :, :], gate[:, 1, :, :], by_token(top[:, 2 + r, :]), ALU.is_equal))
                if r == 0:
                    then(nc.vector.scalar_tensor_tensor(gate[:, 6, :, :], gate[:, mask, :, :], LOWEST, gate[:, 4, :, :], ALU.mult, ALU.add))
            nc.vector.tensor_tensor(top[:, 4, :], top[:, 1, :], top[:, 0, :], ALU.subtract).then_inc(gexp_in, 1)
            dve.wait_ge(gexp_out, 2)
            then(nc.vector.tensor_scalar(top[:, 6, :], top[:, 5, :], 1.0, None, ALU.add))
            then(nc.vector.reciprocal(top[:, 6, :], top[:, 6, :]))
            then(nc.vector.tensor_tensor(top[:, 7, :], top[:, 5, :], top[:, 6, :], ALU.mult))
            then(nc.vector.tensor_tensor(gate[:, 0, :, :], gate[:, 5, :, :], by_token(top[:, 6, :]), ALU.mult))
            then(nc.vector.tensor_tensor(gate[:, 1, :, :], gate[:, 7, :, :], by_token(top[:, 7, :]), ALU.mult))
            then(nc.vector.tensor_tensor(pw[:].rearrange("p e t -> p t e"), gate[:, 0, :, :], gate[:, 1, :, :], ALU.add))
            dve.wait_ge(cs_ld, 16)
            for n in range(16):
                i, c = n // NC, n % NC
                dve.wait_ge(proj_ps, n + 1)
                nc.vector.scalar_tensor_tensor(rotated[i][:, CW * c:CW * c + CW], ps[:, 4 + n % 2, :], mod[:, i // 2:i // 2 + 1],
                                               cs[:, CW * c:CW * c + CW], ALU.mult, ALU.mult).then_inc(rot_ready, 1)

            def add_output(e, c):
                n = e * NC + c
                dve.wait_ge(y_ready, n + 1 + CREDIT)
                dve.wait_ge(y_added, n - NC + 1 + ADDED)
                for k in range(4):
                    t = 4 * c + k
                    ins = nc.vector.scalar_tensor_tensor(acc[:, t, :], ps[:, 4 + c % 2, DM * k:DM * k + DM],
                                                         pw[:, bass.ds(e, 1), t:t + 1].rearrange("p o t -> p (o t)"),
                                                         acc[:, t, :], ALU.mult, ALU.add)
                ins.then_inc(y_added, 1)

            def expert(e):
                for c in range(NC):
                    for f in range(NF):
                        n = e * (NC * NF) + c * NF + f
                        k = c * NF + f
                        rows = FCH[f][1]
                        dve.wait_ge(silu_ready, n + 1 + CREDIT)
                        dve.wait_ge(g_ready, n + 1)
                        if f == 0:
                            dve.wait_ge(y_ready, e * NC + c - 1 + CREDIT)
                        nc.vector.tensor_tensor(hid[0:rows, c % 2, f, :], silu[0:rows, k % 2, :], ps[0:rows, 2 + k % 2, :],
                                                ALU.mult).then_inc(hid_ready, 1)
                        if f == 1 and c > 0:
                            add_output(e, c - 1)
                add_output(e, NC - 1)

            with dve.Fori(0, E // 2) as pr:
                for par in range(2):
                    expert(pr * 2 + par)

            def tile_max(h, i):
                for c in range(NC):
                    m = (h * NT + i) * NC + c
                    dve.wait_ge(m_ready, m + 1)
                    nc.vector.tensor_reduce(m4[:, i, c:c + 1], ps[:, M_BANK + c % 2, :], AX, ALU.max).then_inc(m_reduced, 1)

            def half_max(h, half):
                dve.wait_ge(m_reduced, (h * NT + 8 * half + 8) * NC + CREDIT)
                nc.vector.tensor_reduce(mx[:, half, :], m4[:, 8 * half:8 * half + 8, :], AX, ALU.max).then_inc(mx_ready, 1)

            def make_shift(h, half):
                n = h * 2 + half
                dve.wait_ge(mxT_ready, n + 1)
                dve.wait_ge(shift_ld, n * 32)
                nc.vector.tensor_scalar(shift[:, 0, :], ps[0:8, T_BANK, 0:P], -1.0, None, ALU.mult).then_inc(shift_hi, 1)
                dve.wait_ge(shift_hi, n + 1)
                nc.vector.scalar_tensor_tensor(shift[:, 1, :], ps[0:8, T_BANK, 0:P], -1.0, shift[:, 0, :],
                                               ALU.mult, ALU.subtract).then_inc(shift_ready, 1)

            def normalise(h, u):
                unit = h * 2 + u
                turned = ps[:, T_BANK, :].rearrange("p (b g d) -> p b g d", b=4, g=4)
                dve.wait_ge(ot_ready, unit + 1 + TURNED)
                dve.wait_ge(attn_ready, unit + TURNED)
                nc.vector.tensor_copy(half_sum[:], turned[:, :, 2:4, 0:D + 1]).then_inc(half_ready, 1)
                dve.wait_ge(half_ready, unit + 1)
                nc.vector.tensor_tensor(sums[:], turned[:, :, 0:2, 0:D + 1], half_sum[:], ALU.add).then_inc(sum_ready, 1)
                dve.wait_ge(sum_ready, unit + 1 + TURNED)
                nc.vector.reciprocal(rden[:], sums[:, :, :, D:D + 1]).then_inc(rden_ready, 1)
                dve.wait_ge(rden_ready, unit + 1)
                nc.vector.tensor_tensor(attn[:, 8 * u:8 * u + 8, bass.ds(h * D, D)].rearrange("p (c b) d -> p b c d", c=2),
                                        sums[:, :, :, 0:D], rden[:].to_broadcast([P, 4, 2, D]), ALU.mult).then_inc(attn_ready, 1)

            for i in range(LEAD):
                tile_max(0, i)
                if i == 7:
                    half_max(0, 0)
                if i == 9:
                    make_shift(0, 0)

            def step(h, par, s, first, last):
                if s < 4:
                    tile_max(h, s + LEAD)
                elif not last:
                    tile_max(h + 1, s - 4)
                if s == 3:
                    half_max(h, 1)
                if s == 11 and not last:
                    half_max(h + 1, 0)
                if s == 2 and not first:
                    normalise(h - 1, 1)
                if s == 10:
                    normalise(h, 0)
                if s == 5:
                    make_shift(h, 1)
                if s == 13 and not last:
                    make_shift(h + 1, 0)

            run_steps(dve, step)
            normalise(H - 1, 1)
            for q in range(4):
                dve.wait_ge(fin_ps, q + 1)
                nc.vector.tensor_tensor(acc[:, 4 * q:4 * q + 4, :], acc[:, 4 * q:4 * q + 4, :],
                                        ps[:, 4 + q, :].rearrange("p (t d) -> p t d", t=4), ALU.add).then_inc(fin_ready, 1)

        @block.tensor
        def _(pe):
            pe.sem_inc(y_ready, CREDIT)
            pe.sem_inc(pv_done, CREDIT)
            pe.sem_inc(ot_ready, TURNED)
            pe.wait_ge(ident_ld, 16)
            pe.wait_ge(const_ld, 2 * 16)
            nc.tensor.transpose(ps[:, 2, 0:3 * E], wqkv_sb[:], ident[0:3 * E, 0:3 * E]).then_inc(wqkv_ps, 1)
            for c in range(NC):
                if c >= 2:
                    pe.wait_ge(xt_ready, c - 1)
                for k in range(4):
                    pe.wait_ge(xn_ready, 4 * c + k + 1)
                    ins = nc.tensor.transpose(ps[:, c % 2, P * k:P * k + P], xn[:, 4 * c + k, :], ident[:])
                ins.then_inc(xt_ps, 1)
            pe.wait_ge(wqkv_ready, 1)
            pe.wait_ge(xt_ready, NC)
            for t in range(NT):
                ins = nc.tensor.matmul(ps[:, 3, 3 * E * t:3 * E * t + 3 * E], xnT[:, P * t:P * t + P], wqkvT[:], start=True, stop=True)
            ins.then_inc(mix_ps, 1)
            pe.wait_ge(wmat_ld, 4 * 16)
            pe.wait_ge(wrap_ready, 1)
            for t in range(NT):
                if t % 4 == 0 and t >= 8:
                    pe.wait_ge(v_ready, t // 4 - 1)
                for ahead in range(2):
                    ins = nc.tensor.matmul(ps[:, 6 + t // 4 % 2, DM * (t % 4):DM * (t % 4) + DM],
                                           xnT[:, P * t + ahead:P * t + ahead + P], wmat[:, 2, :], start=ahead == 0, stop=ahead == 1)
                if t % 4 == 3:
                    ins.then_inc(v_ps, 1)

            def expert_weights(e, par):
                pe.wait_ge(w_ld[par], (e - par) * 40 + 80)
                for b in range(NF):
                    bank = 6 + (NF * par + b) % 2
                    pe.wait_ge(wT_ready, e * NF + b - 1 + CREDIT)
                    for f, (f0, n) in enumerate(FCH):
                        if b < 2:
                            ins = nc.tensor.transpose(ps[:, bank, f0:f0 + n], w1raw[0:n, par, NF * b + f, :], ident[0:n, 0:n])
                        else:
                            ins = nc.tensor.transpose(ps[0:n, bank, DM * f:DM * f + DM], w2raw[:, par, f0:f0 + n], ident[:])
                    ins.then_inc(tr_ready, 1)

            pe.wait_ge(v_ready, 4)
            expert_weights(0, 0)
            for n in range(16):
                i, c = n // NC, n % NC
                g, which = i // 2, i % 2
                if n >= 2:
                    pe.wait_ge(rot_ready, n - 1)
                for half in range(2):
                    ins = nc.tensor.matmul(ps[64 * half:64 * half + 64, 4 + n % 2, :], wmat[:, which, 64 * g:64 * g + 64],
                                           xnT[:, CW * c:CW * c + CW], start=True, stop=True, tile_position=(0, 64 * half))
                ins.then_inc(proj_ps, 1)
            pe.wait_ge(rot_ready, 16)

            def expert_out(e, par, c):
                n = e * NC + c
                pe.wait_ge(hid_ready, n * NF + NF + CREDIT)
                pe.wait_ge(y_added, n - 1 + ADDED)
                for k in range(4):
                    for f, (f0, rows) in enumerate(FCH):
                        ins = nc.tensor.matmul(ps[:, 4 + c % 2, DM * k:DM * k + DM], hid[0:rows, c % 2, f, P * k:P * k + P],
                                               w2T[0:rows, par, f, :], start=f == 0, stop=f == NF - 1)
                ins.then_inc(y_ready, 1)

            def expert(e, par, last):
                pe.wait_ge(wT_ready, e * NF + NF + CREDIT)
                for c in range(NC):
                    for f, (f0, rows) in enumerate(FCH):
                        k = c * NF + f
                        n = e * (NC * NF) + k
                        pe.wait_ge(silu_ready, n - 1 + CREDIT)
                        pe.wait_ge(hid_ready, n - 1 + CREDIT)
                        for b, ready in ((0, a_ready), (1, g_ready)):
                            nc.tensor.matmul(ps[0:rows, 2 * b + k % 2, :], w1T[:, par, F * b + f0:F * b + f0 + rows],
                                             xnT[:, CW * c:CW * c + CW], start=True, stop=True).then_inc(ready, 1)
                        if f == 0 and c > 0:
                            expert_out(e, par, c - 1)
                if not last:
                    expert_weights(e + 1, 1 - par)
                expert_out(e, par, NC - 1)

            with pe.Fori(0, E // 2 - 1) as pr:
                for par in range(2):
                    expert(pr * 2 + par, par, False)
            expert(E - 2, 0, False)
            expert(E - 1, 1, True)
            pe.wait_ge(hid_ready, E * NC * NF + CREDIT)
            pe.wait_ge(y_added, E * NC + ADDED)

            def scores(h, par, s):
                g = h * STEPS + s
                u, k = s // 8, s % 8
                if k == 0:
                    pe.wait_ge(shift_ld, (h * 2 + u + 1) * 32)
                for b in range(2):
                    t = 2 * k + b
                    pe.wait_ge(exp_done, g * 2 + b - 1 + CREDIT)
                    for c in range(2):
                        col = CW * (2 * u + c)
                        ins = nc.tensor.matmul(ps[:, SCORE_BANKS + 2 * b + c, :], ka[par][:, P * t:P * t + P],
                                               qa[par][:, col:col + CW], start=True, stop=True)
                    ins.then_inc(score_ready, 1)
                    yield

            def max_scores(h, par, i):
                for c in range(NC):
                    m = (h * NT + i) * NC + c
                    pe.wait_ge(m_reduced, m - 1 + CREDIT)
                    nc.tensor.matmul(ps[:, M_BANK + c % 2, :], qa[par][0:KQ, P * i:P * i + P],
                                     ka[par][0:KQ, CW * c:CW * c + CW], start=True, stop=True).then_inc(m_ready, 1)
                    yield

            def weighted_values(h, par, s):
                g = h * STEPS + s
                u, k = s // 8, s % 8
                if s == 0:
                    pe.wait_ge(vh_ready, h + 1)
                if k == 0:
                    pe.wait_ge(o_copied, h * 2 + u)
                pe.wait_ge(exp_done, g * 2 + 2 + CREDIT)
                for b in range(2):
                    for c in range(2):
                        col = 32 * (2 * b + c)
                        ins = nc.tensor.matmul(ps[col:col + 32, O_BANK, :], vh[:, par, 2 * k + b, :], probs[:, s % 2, b, c, :],
                                               start=k == 0, stop=k == 7, tile_position=(0, col))
                ins.then_inc(pv_done, 1)

            def turn_max(h, half):
                pe.wait_ge(mx_ready, h * 2 + half + 1)
                if not (isinstance(h, int) and h == 0 and half == 0):
                    pe.wait_ge(sum_ready, h * 2 + half - 1 + TURNED)
                nc.tensor.transpose(ps[0:8, T_BANK, 0:P], mx[:, half, :], ident[:]).then_inc(mxT_ready, 1)

            def turn_out(h, u):
                unit = h * 2 + u
                pe.wait_ge(o_copied, unit + 1)
                pe.wait_ge(shift_ready, unit + 1)
                pe.wait_ge(sum_ready, unit + TURNED)
                for b in range(4):
                    ins = nc.tensor.transpose(ps[:, T_BANK, P * b:P * b + P], osb[:, P * b:P * b + P], ident[:])
                ins.then_inc(ot_ready, 1)

            def all_of(gen):
                for _ in gen:
                    pass

            pe.wait_ge(aug_ld, 12 * 16)
            pe.wait_ge(ones_ready, 4)
            for i in range(LEAD):
                all_of(max_scores(0, 0, i))
                if i == 8:
                    turn_max(0, 0)

            def step(h, par, s, first, last):
                if s == 4 and not last:
                    pe.wait_ge(aug_ld, h * 192 + 384)
                sc = scores(h, par, s)
                ms = max_scores(h, par, s + LEAD) if s < 4 else iter(()) if last else max_scores(h + 1, 1 - par, s - 4)
                next(sc)
                next(ms, None)
                next(sc)
                next(ms, None)
                if s > 0:
                    weighted_values(h, par, s - 1)
                elif not first:
                    weighted_values(h - 1, 1 - par, STEPS - 1)
                all_of(sc)
                all_of(ms)
                if s == 2 and not first:
                    turn_out(h - 1, 1)
                if s == 10:
                    turn_out(h, 0)
                if s == 5:
                    turn_max(h, 1)
                if s == 13 and not last:
                    turn_max(h + 1, 0)

            run_steps(pe, step)
            weighted_values(H - 1, 1, STEPS - 1)
            turn_out(H - 1, 1)
            pe.wait_ge(attn_ready, 2 * H + TURNED)
            pe.wait_ge(wo_ready, 1)
            for q in range(4):
                for k in range(4):
                    ins = nc.tensor.transpose(ps[:, q, P * k:P * k + P], attn[:, 4 * q + k, :], ident[:])
                ins.then_inc(at_ps, 1)
            for q in range(4):
                pe.wait_ge(at_ready, q + 1)
                for k in range(4):
                    t = 4 * q + k
                    ins = nc.tensor.matmul(ps[:, 4 + q, DM * k:DM * k + DM], attnT[:, P * t:P * t + P], wo_mod[:], start=True, stop=True)
                ins.then_inc(fin_ps, 1)


_INS = ["L0_attn_x", "L0_attn_Wq", "L0_attn_Wk", "L0_attn_Wv", "L0_attn_Wo", "L0_attn_quantum_phase",
        "L0_attn_quantum_amplitude", "L0_ffn_wqkv", "L0_ffn_w1", "L0_ffn_w2"]


def kernel(**inputs):
    import concourse.bacc as _bacc
    from concourse.bass_utils import run_bass_kernel_spmd as _run

    angle = 2.0 * np.pi * np.arange(S, dtype=np.float64) / S
    rows = np.stack([np.cos(angle), np.sin(angle)]).astype(np.float32)
    shape_constants = {
        "identity": np.eye(P, dtype=np.float32),
        "descending": np.tile(np.arange(E, 0, -1, dtype=np.float32), (P, 1)),
        "cos_sin": np.repeat(rows, P // 2, axis=0),
    }
    nc = _bacc.Bacc("TRN2", target_bir_lowering=False, num_devices=1)
    arrays, args = {}, []
    for name in _INS:
        arrays[f"in_{name}"] = np.ascontiguousarray(inputs[name])
    arrays.update(shape_constants)
    for name, a in arrays.items():
        args.append(nc.dram_tensor(name, a.shape, mybir.dt.from_np(a.dtype), kind="ExternalInput").ap())
    out = nc.dram_tensor("out", (1, S, DM), F32, kind="ExternalOutput").ap()
    build(nc, *args, out)
    result = _run(nc, [arrays], core_ids=[0])
    return result.results[0]["out"]
```

```python
from contextlib import ExitStack

import numpy as np

import concourse.bass as bass
from concourse import mybir

F32 = mybir.dt.float32
BF16 = mybir.dt.bfloat16
ALU = mybir.AluOpType
ACT = mybir.ActivationFunctionType
AX = mybir.AxisListType.X

P = 128
S = 2048
DM = 128
H = 16
D = 8
E = 8
F = 352
NT = S // P
CW = 512
NC = S // CW
FCH = [(0, 128), (128, 128), (256, 96)]
NF = len(FCH)
ROWS = 2 * D
KQ = 6 * ROWS
KS = KQ + 2
STEPS = NT
CREDIT = 2
PBUFS = 4
PV_LAG = 2
TURNED = 1
ADDED = NC
ISQ8 = float(1.0 / np.sqrt(D))
TWO_PI = 2.0 * np.pi
PI_A = 6.28125
PI_B = float(np.float32(2.0 ** -20 * np.floor((TWO_PI - PI_A) * 2.0 ** 20)))
PI_C = float(TWO_PI - PI_A - PI_B)
ROUND = 12582912.0
PI_DOWN = 3.1415925
LOWEST = -3.0e38
EPS = 1e-5
SCORE_BANKS, O_BANK, T_BANK, M_BANK = 0, 4, 5, 6
SPAN, BELOW = 130.0, 62.0
SQ8 = float(np.sqrt(D))
SLACK = 1.02
LEAD = 12


def build(nc, x, Wq, Wk, Wv, Wo, phase, amp, wqkv, w1, w2, ident_in, desc_in, cs_in, sel_in, out):
    scratch = nc.dram_tensor("qk_parts", [2, 3, H, ROWS, S], BF16, kind="Internal").ap()
    x_v = x.rearrange("a (t p) d -> p (a t) d", p=P)
    out_v = out.rearrange("a (t p) d -> p (a t) d", p=P)

    with ExitStack() as ctx:
        def sb(name, shape, dt):
            return ctx.enter_context(nc.sbuf_tensor(name, shape, dt))

        def sem(name):
            return ctx.enter_context(nc.semaphore(name))

        acc = sb("acc", [P, NT, DM], F32)
        xnT = sb("xnT", [P, S + 1], F32)
        big = sb("big", [P, 4, S], F32)
        rotated = [big[:, i, :] for i in range(4)]
        xn = big[:, 3, :].rearrange("p (t d) -> p t d", d=DM)
        probs = big[:].rearrange("p a (b c n) -> p a b c n", b=2, c=2)
        parts = sb("parts", [P, 4, 3, S], BF16)
        attn = parts[:, 1, 0:2, :].rearrange("p a n -> p (a n)").bitcast(F32).rearrange("p (t d) -> p t d", d=DM)
        cs = sb("cs", [P, S], F32)
        ident = sb("ident", [P, P], F32)
        desc = sb("desc", [P, E], F32)
        sel = sb("sel", [P, 8], F32)
        sel16 = sb("sel16", [P, 3, 8], BF16)
        squares = [big[:, i, 0:S // 2].bitcast(BF16) for i in range(4)]
        kmean = sb("kmean", [P, 2], F32)
        ones = sb("ones", [P, P], F32)
        knorm = sb("knorm", [P, 2, H], F32)
        kdiag = sb("kdiag", [H, 2, H], F32)
        bound = sb("bound", [P, 3, NT, H], F32)
        use_max = sb("use_max", [P, H], F32)
        flags = sb("flags", [1, H], mybir.dt.int32)
        other = sb("other", [P, H, NT], F32)
        wmat = sb("wmat", [P, 4, DM], F32)
        wo_mod = sb("wo_mod", [P, DM], F32)
        wqkv_sb = sb("wqkv_sb", [3 * E, DM], F32)
        wqkvT = sb("wqkvT", [P, 3 * E], F32)
        stats = sb("stats", [P, NT, 6], F32)
        mv = sb("mv", [P, NT, 2], F32)
        ve = sb("ve", [P, 4, NT], F32)
        rstd = sb("rstd", [P, NT], F32)
        ang = sb("ang", [P, 8, 3], F32)
        mod = sb("mod", [P, 3], F32)
        mix = sb("mix", [P, NT, 3 * E], F32)
        pair = sb("pair", [P, NT, E, E], F32)
        gate = sb("gate", [P, 8, NT, E], F32)
        top = sb("top", [P, 8, NT], F32)
        pw = sb("pw", [P, E, NT], F32)
        w1raw = sb("w1raw", [P, 2, 2 * NF, DM], F32)
        w2raw = sb("w2raw", [P, 2, F], F32)
        w1T = sb("w1T", [P, 2, 2 * F], F32)
        w2T = sb("w2T", [P, 2, NF, DM], F32)
        silu = sb("silu", [P, 2, CW], F32)
        hid = sb("hid", [P, 2, NF, CW], F32)
        vaug = sb("vaug", [P, H, NT, D + 1], F32)
        vh = sb("vh", [P, 2, NT, 32], F32)
        qa = [sb(f"qa{i}", [KS, S], BF16) for i in range(2)]
        ka = [sb(f"ka{i}", [KS, S], BF16) for i in range(2)]
        m4 = sb("m4", [P, NT, NC], F32)
        mx = sb("mx", [P, 2, 8], F32)
        shift = sb("shift", [8, 2, P], BF16)
        osb = sb("osb", [P, CW], F32)
        half_sum = sb("half_sum", [P, 4, 2, D + 1], F32)
        sums = sb("sums", [P, 4, 2, D + 1], F32)
        rden = sb("rden", [P, 4, 2, 1], F32)
        attnT = sb("attnT", [P, S], F32)
        ps = ctx.enter_context(nc.psum_tensor("ps", [P, 8, CW], F32))

        x_in = [sem(f"x_in{i}") for i in range(4)]
        ident_ld, const_ld, wmat_ld, phase_ld, cs_ld = (sem(n) for n in ("ident_ld", "const_ld", "wmat_ld", "phase_ld", "cs_ld"))
        w_ld = [sem(f"w_ld{i}") for i in range(2)]
        dve_step, var_ready, sd_ready, xn_ready = (sem(n) for n in ("dve_step", "var_ready", "sd_ready", "xn_ready"))
        xt_ps, xt_ready, wrap_ready = (sem(n) for n in ("xt_ps", "xt_ready", "wrap_ready"))
        ang_ready, sin_ready, mod_ready = (sem(n) for n in ("ang_ready", "sin_ready", "mod_ready"))
        wqkv_ps, wqkv_ready, mix_ps, mix_ready = (sem(n) for n in ("wqkv_ps", "wqkv_ready", "mix_ps", "mix_ready"))
        gexp_in, gexp_out, pw_ready = (sem(n) for n in ("gexp_in", "gexp_out", "pw_ready"))
        norm_parts, kmean_ready = sem("norm_parts"), sem("kmean_ready")
        proj_ps, rot_ready, v_ps, v_ready, ones_ready = (sem(n) for n in ("proj_ps", "rot_ready", "v_ps", "v_ready", "ones_ready"))
        split_step, parts_ready, scratch_wr = (sem(n) for n in ("split_step", "parts_ready", "scratch_wr"))
        norms_ps, kmax_in, kmaxT_ps, kdiag_ready, kmax_ps, use_ready, use_ps, flags_ready = (
            sem(n) for n in ("norms_ps", "kmax_in", "kmaxT_ps", "kdiag_ready", "kmax_ps", "use_ready", "use_ps", "flags_ready"))
        tr_ready, wT_ready = sem("tr_ready"), sem("wT_ready")
        a_ready, g_ready, silu_ready, hid_ready, y_ready, y_added = (
            sem(n) for n in ("a_ready", "g_ready", "silu_ready", "hid_ready", "y_ready", "y_added"))
        aug_ld, score_ready, exp_done, pv_done, vh_ready = (
            sem(n) for n in ("aug_ld", "score_ready", "exp_done", "pv_done", "vh_ready"))
        m_ready, m_reduced, mx_ready, mxT_ready, shift_hi, shift_ready, shift_ld = (
            sem(n) for n in ("m_ready", "m_reduced", "mx_ready", "mxT_ready", "shift_hi", "shift_ready", "shift_ld"))
        o_copied, ot_ready, half_ready, sum_ready, rden_ready, attn_ready = (
            sem(n) for n in ("o_copied", "ot_ready", "half_ready", "sum_ready", "rden_ready", "attn_ready"))
        at_ps, at_ready, fin_ps, fin_ready, out_wr, wo_ready = (
            sem(n) for n in ("at_ps", "at_ready", "fin_ps", "fin_ready", "out_wr", "wo_ready"))

        block = ctx.enter_context(nc.Block())

        def part_a(h, par):
            return [(h, par, t) for t in range(NT - LEAD)]

        def part_b(h, par):
            return [(h, par, t) for t in range(NT - LEAD, STEPS)]

        def run_heads(eng, run):
            run("a", part_a(0, 0), True, False)
            with eng.Fori(0, H // 2 - 1) as pr:
                for par in range(2):
                    run("b", part_b(pr * 2 + par, par), False, False)
                    run("a", part_a(pr * 2 + par + 1, 1 - par), False, False)
            run("b", part_b(H - 2, 0), False, False)
            run("a", part_a(H - 1, 1), False, True)
            run("b", part_b(H - 1, 1), False, True)

        def run_steps(eng, step):
            def run(part, steps, first, last):
                for h, par, t in steps:
                    step(h, par, t, first, last)
            run_heads(eng, run)

        @block.sync
        def _(sp):
            for i in range(4):
                sp.dma_start(acc[:, 4 * i:4 * i + 4, :], x_v[:, 4 * i:4 * i + 4, :]).then_inc(x_in[i], 16)
            sp.dma_start(ident[:], ident_in).then_inc(ident_ld, 16)
            sp.dma_start(desc[:], desc_in).then_inc(const_ld, 16)
            sp.dma_start(sel[:], sel_in).then_inc(const_ld, 16)
            sp.dma_start(wqkv_sb[:], wqkv).then_inc(const_ld, 16)
            for i, w in enumerate((Wq, Wk, Wv, Wo)):
                sp.dma_start(wmat[:, i, :], w).then_inc(wmat_ld, 16)
            for src, at in ((phase, 0), (amp, 1)):
                for g in range(2):
                    for half in range(2):
                        sp.dma_start(ang[64 * half:64 * half + 64, at, g:g + 1],
                                     src[8 * g:8 * g + 8, :].rearrange("h (d o) -> (h d) o", o=1)).then_inc(phase_ld, 16)
                sp.dma_start(ang[:, at, 2:3], src.rearrange("h (d o) -> (h d) o", o=1)).then_inc(phase_ld, 16)

            def load_expert(e, par):
                for b in range(2):
                    sp.dma_start(w1raw[:, par, NF * b:NF * b + 2, :],
                                 w1[e, F * b:F * b + 256, :].rearrange("(c p) h -> p c h", p=P)).then_inc(w_ld[par], 16)
                    sp.dma_start(w1raw[0:96, par, NF * b + 2, :], w1[e, F * b + 256:F * b + F, :]).then_inc(w_ld[par], 16)
                sp.dma_start(w2raw[:, par, :], w2[e]).then_inc(w_ld[par], 16)

            load_expert(0, 0)
            load_expert(1, 1)
            sp.dma_start(cs[:], cs_in).then_inc(cs_ld, 16)
            with sp.Fori(0, E // 2 - 1) as pr:
                for par in range(2):
                    e = pr * 2 + par
                    sp.wait_ge(tr_ready, e * NF + NF)
                    load_expert(e + 2, par)

            for i in range(4):
                sp.wait_ge(parts_ready, i + 1)
                g, which = i // 2, i % 2
                for part in range(3):
                    for half in range(2):
                        sp.dma_start(scratch[which, part, 8 * g:8 * g + 8, 8 * half:8 * half + 8, :],
                                     parts[64 * half:64 * half + 64, i, part, :]).then_inc(scratch_wr, 16)
            sp.wait_ge(scratch_wr, 24 * 16)

            def load_head(h, par):
                q_parts, k_parts = (0, 0, 0, 1, 1, 2), (0, 1, 2, 0, 1, 0)
                for buf, which, order in ((qa[par], 0, q_parts), (ka[par], 1, k_parts)):
                    for b, part in enumerate(order):
                        sp.dma_start(buf[ROWS * b:ROWS * b + ROWS, :], scratch[which, part, h, :, :]).then_inc(aug_ld, 16)

            def load_shift(h, par, half):
                sp.wait_ge(shift_ready, h * 2 + half + 1)
                for r in range(2):
                    sp.dma_start(qa[par][KQ + r:KQ + r + 1, 1024 * half:1024 * half + 1024].rearrange("o (t p) -> o t p", p=P),
                                 shift[:, r, :]).then_inc(shift_ld, 16)

            load_head(0, 0)
            load_shift(0, 0, 0)

            def step(h, par, s, first, last):
                if s == 0 and not last:
                    sp.wait_ge(score_ready, h * (2 * STEPS))
                    load_head(h + 1, 1 - par)
                if s == 5:
                    load_shift(h, par, 1)
                if s == 13 and not last:
                    load_shift(h + 1, 1 - par, 0)

            run_steps(sp, step)
            for q in range(4):
                sp.wait_ge(fin_ready, q + 1)
                sp.dma_start(out_v[:, 4 * q:4 * q + 4, :], acc[:, 4 * q:4 * q + 4, :]).then_inc(out_wr, 16)
            sp.wait_ge(out_wr, 4 * 16)

        @block.gpsimd
        def _(pool):
            nc.gpsimd.memset(vaug[:], 1.0).then_inc(ones_ready, 1)
            nc.gpsimd.memset(vh[:], 0.0).then_inc(ones_ready, 1)
            pool.wait_ge(const_ld, 3 * 16)
            nc.gpsimd.tensor_copy(sel16[:, 0, :], sel[:]).then_inc(norm_parts, 1)
            done = 0
            for i in range(4):
                pool.wait_ge(rot_ready, 4 * (i + 1))
                for part in range(3):
                    nc.gpsimd.tensor_copy(parts[:, i, part, :], rotated[i]).then_inc(split_step if part < 2 else parts_ready, 1)
                    if part == 2:
                        pool.wait_ge(parts_ready, i + 1)
                    if part < 2:
                        done += 1
                        pool.wait_ge(split_step, done)
                        nc.gpsimd.tensor_tensor(rotated[i], rotated[i], parts[:, i, part, :], ALU.subtract).then_inc(split_step, 1)
                        done += 1
                        pool.wait_ge(split_step, done)

                hi = parts[:, i, 0, :]
                nc.gpsimd.tensor_tensor(squares[i], hi, hi, ALU.mult).then_inc(norm_parts, 1)

            def head_values(h, par):
                nc.gpsimd.tensor_copy(vh[:, par, :, 0:D + 1], vaug[:, bass.ds(h, 1), :, :].rearrange("p o t d -> p (o t) d")).then_inc(vh_ready, 1)

            pool.wait_ge(v_ready, 4)
            pool.wait_ge(ones_ready, 5)
            head_values(0, 0)

            def step(h, par, s, first, last):
                if s == 1 and not last:
                    pool.wait_ge(pv_done, h * STEPS + PBUFS)
                    head_values(h + 1, 1 - par)

            run_steps(pool, step)

        @block.scalar
        def _(act):
            act.sem_inc(wT_ready, CREDIT)
            act.sem_inc(silu_ready, CREDIT)
            act.sem_inc(exp_done, CREDIT)
            act.wait_ge(var_ready, 1)
            nc.scalar.activation(ve[:, 1, :], ve[:, 0, :], ACT.Sqrt).then_inc(sd_ready, 1)
            act.wait_ge(ang_ready, 1)
            nc.scalar.activation(ang[:, 5, :], ang[:, 4, :], ACT.Sin, scale=0.5).then_inc(sin_ready, 1)
            act.wait_ge(wqkv_ps, 1)
            nc.scalar.copy(wqkvT[:], ps[:, 2, 0:3 * E]).then_inc(wqkv_ready, 1)
            for c in range(NC):
                act.wait_ge(xt_ps, c + 1)
                nc.scalar.copy(xnT[:, CW * c:CW * c + CW], ps[:, c % 2, :]).then_inc(xt_ready, 1)
            act.wait_ge(xt_ready, 1)
            nc.scalar.copy(xnT[:, S:S + 1], xnT[:, 0:1]).then_inc(wrap_ready, 1)
            act.wait_ge(ones_ready, 5)
            for q in range(4):
                act.wait_ge(v_ps, q + 1)
                nc.scalar.copy(vaug[:, :, 4 * q:4 * q + 4, 0:D],
                               ps[:, 6 + q % 2, :].rearrange("p (t h d) -> p h t d", t=4, h=H)).then_inc(v_ready, 1)

            def expert_weights(e, par):
                for b in range(NF):
                    act.wait_ge(tr_ready, e * NF + b + 1)
                    bank = 6 + (NF * par + b) % 2
                    if b < 2:
                        nc.scalar.copy(w1T[:, par, F * b:F * b + F], ps[:, bank, 0:F]).then_inc(wT_ready, 1)
                    else:
                        nc.scalar.copy(w2T[:, par, 0:2, :], ps[:, bank, 0:2 * DM].rearrange("p (c h) -> p c h", h=DM))
                        nc.scalar.copy(w2T[0:96, par, 2, :], ps[0:96, bank, 2 * DM:3 * DM]).then_inc(wT_ready, 1)

            expert_weights(0, 0)
            for r in range(2):
                act.wait_ge(gexp_in, r + 1)
                if r == 0:
                    nc.scalar.activation(pair[:], pair[:], ACT.Exp).then_inc(gexp_out, 1)
                else:
                    nc.scalar.activation(top[:, 5, :], top[:, 4, :], ACT.Exp).then_inc(gexp_out, 1)

            def expert(e, par, last):
                for k in range(NC * NF):
                    f = k % NF
                    n = e * (NC * NF) + k
                    rows = FCH[f][1]
                    act.wait_ge(a_ready, n + 1)
                    act.wait_ge(hid_ready, n - 1 + CREDIT)
                    nc.scalar.activation(silu[0:rows, k % 2, :], ps[0:rows, k % 2, :], ACT.Silu).then_inc(silu_ready, 1)
                if not last:
                    expert_weights(e + 1, 1 - par)

            with act.Fori(0, E // 2 - 1) as pr:
                for par in range(2):
                    expert(pr * 2 + par, par, False)
            expert(E - 2, 0, False)
            expert(E - 1, 1, True)

            def copy_out(unit, steps_done):
                act.wait_ge(pv_done, steps_done + PBUFS)
                act.wait_ge(ot_ready, unit + TURNED)
                nc.scalar.copy(osb[:], ps[:, O_BANK, :]).then_inc(o_copied, 1)

            def step(h, par, s, first, last):
                g = h * STEPS + s
                for b in range(2):
                    act.wait_ge(score_ready, g * 2 + b + 1)
                    act.wait_ge(pv_done, g + 1)
                    nc.scalar.activation(probs[:, s % PBUFS, b, :, :], ps[:, 2 * b:2 * b + 2, :], ACT.Exp, scale=ISQ8).then_inc(exp_done, 1)
                if s == PV_LAG - 1 and not first:
                    copy_out(h * 2 - 1, h * STEPS)
                if s == 8 + PV_LAG - 1:
                    copy_out(h * 2, h * STEPS + 8)

            run_steps(act, step)
            copy_out(2 * H - 1, H * STEPS)
            for q in range(4):
                act.wait_ge(at_ps, q + 1)
                nc.scalar.copy(attnT[:, CW * q:CW * q + CW], ps[:, q, :]).then_inc(at_ready, 1)

        @block.vector
        def _(dve):
            chain = [0]

            def then(ins):
                chain[0] += 1
                ins.then_inc(dve_step, 1)
                dve.wait_ge(dve_step, chain[0])

            dve.sem_inc(m_reduced, CREDIT)
            dve.sem_inc(sum_ready, TURNED)
            dve.sem_inc(attn_ready, TURNED)
            dve.sem_inc(hid_ready, CREDIT)
            dve.sem_inc(y_added, ADDED)
            nc.vector.memset(ones[:], 1.0).then_inc(ones_ready, 1)
            for i in range(2):
                nc.vector.memset(ka[i][KQ:KS, :], 1.0).then_inc(ones_ready, 1)
            for t in range(NT):
                if t % 4 == 0:
                    dve.wait_ge(x_in[t // 4], 16)
                ins = nc.vector.bn_stats(stats[:, t, :], acc[:, t, :])
            then(ins)
            for t in range(NT):
                ins = nc.vector.bn_aggr(mv[:, t, :], stats[:, t, :])
            then(ins)
            nc.vector.tensor_scalar(ve[:, 0, :], mv[:, :, 1], EPS, None, ALU.add).then_inc(var_ready, 1)
            dve.wait_ge(sd_ready, 1)
            then(nc.vector.reciprocal(rstd[:], ve[:, 1, :]))
            then(nc.vector.tensor_tensor(ve[:, 2, :], rstd[:], rstd[:], ALU.mult))
            then(nc.vector.tensor_tensor(ve[:, 3, :], ve[:, 2, :], ve[:, 0, :], ALU.mult))
            then(nc.vector.tensor_scalar(ve[:, 2, :], ve[:, 3, :], -0.5, 1.5, ALU.mult, ALU.add))
            then(nc.vector.tensor_tensor(rstd[:], rstd[:], ve[:, 2, :], ALU.mult))
            for t in range(NT):
                nc.vector.tensor_scalar(xn[:, t, :], acc[:, t, :], mv[:, t, 0:1], rstd[:, t:t + 1],
                                        ALU.subtract, ALU.mult).then_inc(xn_ready, 1)
            dve.wait_ge(phase_ld, 10 * 16)
            then(nc.vector.tensor_scalar(ang[:, 2, :], ang[:, 0, :], float(1.0 / TWO_PI), ROUND, ALU.mult, ALU.add))
            then(nc.vector.tensor_scalar(ang[:, 3, :], ang[:, 2, :], ROUND, None, ALU.subtract))
            then(nc.vector.scalar_tensor_tensor(ang[:, 4, :], ang[:, 3, :], -PI_A, ang[:, 0, :], ALU.mult, ALU.add))
            then(nc.vector.scalar_tensor_tensor(ang[:, 6, :], ang[:, 3, :], -PI_B, ang[:, 4, :], ALU.mult, ALU.add))
            then(nc.vector.scalar_tensor_tensor(ang[:, 7, :], ang[:, 3, :], -PI_C, ang[:, 6, :], ALU.mult, ALU.add))
            nc.vector.tensor_scalar(ang[:, 4, :], ang[:, 7, :], PI_DOWN, -PI_DOWN, ALU.min, ALU.max).then_inc(ang_ready, 1)
            dve.wait_ge(sin_ready, 1)
            then(nc.vector.tensor_tensor(ang[:, 6, :], ang[:, 5, :], ang[:, 5, :], ALU.mult))
            then(nc.vector.tensor_scalar(ang[:, 7, :], ang[:, 6, :], -2.0, 1.0, ALU.mult, ALU.add))
            then(nc.vector.tensor_tensor(mod[:], ang[:, 7, :], ang[:, 1, :], ALU.mult))
            dve.wait_ge(wmat_ld, 4 * 16)
            nc.vector.tensor_scalar(wo_mod[:], wmat[:, 3, :], mod[:, 2:3], float(1.0 / np.sqrt(2.0)), ALU.mult, ALU.mult).then_inc(wo_ready, 1)

            def over_j(ap):
                return ap.unsqueeze(3).to_broadcast([P, NT, E, E])

            def over_e(ap):
                return ap.unsqueeze(2).to_broadcast([P, NT, E, E])

            def by_token(ap):
                return ap.unsqueeze(2).to_broadcast([P, NT, E])

            dve.wait_ge(mix_ps, 1)
            then(nc.vector.tensor_copy(mix[:], ps[:, 3, 0:NT * 3 * E].rearrange("p (t n) -> p t n", t=NT)))
            then(nc.vector.tensor_tensor(pair[:], over_j(mix[:, :, 0:E]), over_e(mix[:, :, E:2 * E]), ALU.mult))
            then(nc.vector.tensor_reduce(gate[:, 0, :, :], pair[:], AX, ALU.max))
            nc.vector.tensor_tensor(pair[:], pair[:], over_j(gate[:, 0, :, :]), ALU.subtract).then_inc(gexp_in, 1)
            dve.wait_ge(gexp_out, 1)
            then(nc.vector.tensor_reduce(gate[:, 1, :, :], pair[:], AX, ALU.add))
            then(nc.vector.tensor_tensor(pair[:], pair[:], over_e(mix[:, :, 2 * E:3 * E]), ALU.mult))
            then(nc.vector.tensor_reduce(gate[:, 2, :, :], pair[:], AX, ALU.add))
            then(nc.vector.reciprocal(gate[:, 3, :, :], gate[:, 1, :, :]))
            then(nc.vector.tensor_tensor(gate[:, 4, :, :], gate[:, 2, :, :], gate[:, 3, :, :], ALU.mult))
            dve.wait_ge(const_ld, 3 * 16)
            order = desc[:].unsqueeze(1).to_broadcast([P, NT, E])
            for r, (logits, mask) in enumerate(((4, 5), (6, 7))):
                then(nc.vector.tensor_reduce(top[:, r, :], gate[:, logits, :, :], AX, ALU.max))
                then(nc.vector.tensor_tensor(gate[:, 0, :, :], gate[:, logits, :, :], by_token(top[:, r, :]), ALU.is_equal))
                then(nc.vector.tensor_tensor(gate[:, 1, :, :], gate[:, 0, :, :], order, ALU.mult))
                then(nc.vector.tensor_reduce(top[:, 2 + r, :], gate[:, 1, :, :], AX, ALU.max))
                then(nc.vector.tensor_tensor(gate[:, mask, :, :], gate[:, 1, :, :], by_token(top[:, 2 + r, :]), ALU.is_equal))
                if r == 0:
                    then(nc.vector.scalar_tensor_tensor(gate[:, 6, :, :], gate[:, mask, :, :], LOWEST, gate[:, 4, :, :], ALU.mult, ALU.add))
            nc.vector.tensor_tensor(top[:, 4, :], top[:, 1, :], top[:, 0, :], ALU.subtract).then_inc(gexp_in, 1)
            dve.wait_ge(gexp_out, 2)
            then(nc.vector.tensor_scalar(top[:, 6, :], top[:, 5, :], 1.0, None, ALU.add))
            then(nc.vector.reciprocal(top[:, 6, :], top[:, 6, :]))
            then(nc.vector.tensor_tensor(top[:, 7, :], top[:, 5, :], top[:, 6, :], ALU.mult))
            then(nc.vector.tensor_tensor(gate[:, 0, :, :], gate[:, 5, :, :], by_token(top[:, 6, :]), ALU.mult))
            then(nc.vector.tensor_tensor(gate[:, 1, :, :], gate[:, 7, :, :], by_token(top[:, 7, :]), ALU.mult))
            then(nc.vector.tensor_tensor(pw[:].rearrange("p e t -> p t e"), gate[:, 0, :, :], gate[:, 1, :, :], ALU.add))
            dve.wait_ge(cs_ld, 16)
            for n in range(16):
                i, c = n // NC, n % NC
                dve.wait_ge(proj_ps, n + 1)
                nc.vector.scalar_tensor_tensor(rotated[i][:, CW * c:CW * c + CW], ps[:, 4 + n % 2, :], mod[:, i // 2:i // 2 + 1],
                                               cs[:, CW * c:CW * c + CW], ALU.mult, ALU.mult).then_inc(rot_ready, 1)

            def add_output(e, c):
                n = e * NC + c
                dve.wait_ge(y_ready, n + 1 + CREDIT)
                dve.wait_ge(y_added, n - NC + 1 + ADDED)
                for k in range(4):
                    t = 4 * c + k
                    ins = nc.vector.scalar_tensor_tensor(acc[:, t, :], ps[:, 4 + c % 2, DM * k:DM * k + DM],
                                                         pw[:, bass.ds(e, 1), t:t + 1].rearrange("p o t -> p (o t)"),
                                                         acc[:, t, :], ALU.mult, ALU.add)
                ins.then_inc(y_added, 1)

            def expert(e):
                for c in range(NC):
                    for f in range(NF):
                        n = e * (NC * NF) + c * NF + f
                        k = c * NF + f
                        rows = FCH[f][1]
                        dve.wait_ge(silu_ready, n + 1 + CREDIT)
                        dve.wait_ge(g_ready, n + 1)
                        if f == 0:
                            dve.wait_ge(y_ready, e * NC + c - 1 + CREDIT)
                        nc.vector.tensor_tensor(hid[0:rows, c % 2, f, :], silu[0:rows, k % 2, :], ps[0:rows, 2 + k % 2, :],
                                                ALU.mult).then_inc(hid_ready, 1)
                        if f == 1 and c > 0:
                            add_output(e, c - 1)
                add_output(e, NC - 1)

            with dve.Fori(0, E // 2 - 1) as pr:
                for par in range(2):
                    expert(pr * 2 + par)

            dve.wait_ge(norm_parts, 5)
            for g in range(2):
                then(nc.vector.tensor_reduce(kmean[:, g:g + 1], parts[:, 2 * g + 1, 0, :], AX, ALU.add))
                nc.vector.tensor_scalar(sel16[:, 1 + g, :], sel[:], kmean[:, g:g + 1], 1.0 / S, ALU.mult, ALU.mult).then_inc(kmean_ready, 1)
            dve.wait_ge(norms_ps, 1)
            q_norm = ps[:, 7, 0:NT * H].rearrange("p (t h) -> p t h", t=NT)
            k_norm = ps[:, 7, NT * H:2 * NT * H].rearrange("p (t h) -> p h t", t=NT)
            mean = ps[:, 6, 0:NT * H].rearrange("p (t h) -> p t h", t=NT)
            then(nc.vector.tensor_scalar(bound[:, 0, :, :], mean, SPAN * SQ8, 0.0, ALU.add, ALU.max))
            then(nc.vector.tensor_scalar(other[:].rearrange("p h t -> p t h"), mean, BELOW * SQ8, None, ALU.add))
            nc.vector.tensor_reduce(knorm[:, 0, :], k_norm, AX, ALU.max).then_inc(kmax_in, 1)
            dve.wait_ge(kmaxT_ps, 1)
            then(nc.vector.tensor_reduce(kdiag[:, 1, 0:1], ps[0:H, 6, 256:256 + P], AX, ALU.max))
            nc.vector.tensor_scalar(kdiag[:, 0, :], ident[0:H, 0:H], kdiag[:, 1, 0:1], SLACK * SLACK, ALU.mult, ALU.mult).then_inc(kdiag_ready, 1)
            then(nc.vector.tensor_tensor(bound[:, 1, :, :], bound[:, 0, :, :], bound[:, 0, :, :], ALU.mult))
            dve.wait_ge(kmax_ps, 1)
            then(nc.vector.tensor_copy(knorm[:, 1, :], ps[:, 6, 384:384 + H]))
            then(nc.vector.tensor_tensor(bound[:, 2, :, :], q_norm, knorm[:, 1, :].unsqueeze(1).to_broadcast([P, NT, H]), ALU.mult))
            then(nc.vector.tensor_tensor(bound[:, 0, :, :], bound[:, 2, :, :], bound[:, 1, :, :], ALU.is_gt))
            nc.vector.tensor_reduce(use_max[:], bound[:, 0, :, :].rearrange("p t h -> p h t"), AX, ALU.max).then_inc(use_ready, 1)
            dve.wait_ge(use_ps, 1)
            nc.vector.tensor_copy(flags[:], ps[0:1, 6, 400:400 + H]).then_inc(flags_ready, 1)
            for e in range(E - 2, E):
                expert(e)

            def tile_max(h, i, between=iter(())):
                for c in range(NC):
                    m = (h * NT + i) * NC + c
                    dve.wait_ge(m_ready, m + 1)
                    nc.vector.tensor_reduce(m4[:, i, c:c + 1], ps[:, M_BANK + c % 2, :], AX, ALU.max).then_inc(m_reduced, 1)
                    next(between, None)

            def half_max(h, half):
                dve.wait_ge(m_reduced, (h * NT + 8 * half + 8) * NC + CREDIT)
                nc.vector.tensor_reduce(mx[:, half, :], m4[:, 8 * half:8 * half + 8, :], AX, ALU.max).then_inc(mx_ready, 1)

            def make_shift(h, half):
                n = h * 2 + half
                dve.wait_ge(mxT_ready, n + 1)
                dve.wait_ge(shift_ld, n * 32)
                nc.vector.tensor_scalar(shift[:, 0, :], ps[0:8, T_BANK, 0:P], -1.0, None, ALU.mult).then_inc(shift_hi, 1)
                yield
                dve.wait_ge(shift_hi, n + 1)
                nc.vector.scalar_tensor_tensor(shift[:, 1, :], ps[0:8, T_BANK, 0:P], -1.0, shift[:, 0, :],
                                               ALU.mult, ALU.subtract).then_inc(shift_ready, 1)
                yield

            def normalise(h, u):
                unit = h * 2 + u
                turned = ps[:, T_BANK, :].rearrange("p (b g d) -> p b g d", b=4, g=4)
                dve.wait_ge(ot_ready, unit + 1 + TURNED)
                dve.wait_ge(attn_ready, unit + TURNED)
                nc.vector.tensor_copy(half_sum[:], turned[:, :, 2:4, 0:D + 1]).then_inc(half_ready, 1)
                yield
                dve.wait_ge(half_ready, unit + 1)
                nc.vector.tensor_tensor(sums[:], turned[:, :, 0:2, 0:D + 1], half_sum[:], ALU.add).then_inc(sum_ready, 1)
                yield
                dve.wait_ge(sum_ready, unit + 1 + TURNED)
                nc.vector.reciprocal(rden[:], sums[:, :, :, D:D + 1]).then_inc(rden_ready, 1)
                yield
                dve.wait_ge(rden_ready, unit + 1)
                nc.vector.tensor_tensor(attn[:, 8 * u:8 * u + 8, bass.ds(h * D, D)].rearrange("p (c b) d -> p b c d", c=2),
                                        sums[:, :, :, 0:D], rden[:].to_broadcast([P, 4, 2, D]), ALU.mult).then_inc(attn_ready, 1)
                yield

            def no_max(h, i0, n):
                if not (isinstance(h, int) and h == 0):
                    dve.wait_ge(mx_ready, h * 2)
                nc.vector.tensor_copy(m4[:, i0:i0 + n, :], other[:, bass.ds(h, 1), i0:i0 + n].rearrange("p o t -> p (o t)")
                                      .unsqueeze(2).to_broadcast([P, n, NC])).then_inc(m_reduced, n * NC)

            dve.wait_ge(flags_ready, 1)
            need = dve.value_load(flags[0:1, 0:1], min_val=0, max_val=P)
            with dve.If(need != 0):
                for i in range(LEAD):
                    tile_max(0, i)
            with dve.Else():
                no_max(0, 0, LEAD)
            half_max(0, 0)
            for _ in make_shift(0, 0):
                pass

            def step(h, par, s, first, last, with_max):
                beside = iter(())
                if s == 3 and not first:
                    beside = normalise(h - 1, 1)
                if s == 11:
                    beside = normalise(h, 0)
                if s == 6:
                    beside = make_shift(h, 1)
                if s == 14 and not last:
                    beside = make_shift(h + 1, 0)
                if with_max and s < 4:
                    tile_max(h, s + LEAD, beside)
                elif with_max:
                    tile_max(h + 1, s - 4, beside)
                for _ in beside:
                    pass
                if s == 3:
                    half_max(h, 1)
                if s == 11 and not last:
                    half_max(h + 1, 0)

            flag = [need]

            def run(part, steps, first, last):
                h = steps[0][0]
                if part == "b" and not last:
                    flag[0] = dve.value_load(flags[0:1, bass.ds(h + 1, 1)], min_val=0, max_val=P)
                if part == "b" and last:
                    for h, par, t in steps:
                        step(h, par, t, first, last, False)
                    return
                with dve.If(flag[0] != 0):
                    for h, par, t in steps:
                        step(h, par, t, first, last, True)
                with dve.Else():
                    if part == "a":
                        no_max(h, LEAD, NT - LEAD)
                    else:
                        no_max(h + 1, 0, LEAD)
                    for h, par, t in steps:
                        step(h, par, t, first, last, False)

            run_heads(dve, run)
            for _ in normalise(H - 1, 1):
                pass
            for q in range(4):
                dve.wait_ge(fin_ps, q + 1)
                nc.vector.tensor_tensor(acc[:, 4 * q:4 * q + 4, :], acc[:, 4 * q:4 * q + 4, :],
                                        ps[:, 4 + q, :].rearrange("p (t d) -> p t d", t=4), ALU.add).then_inc(fin_ready, 1)

        @block.tensor
        def _(pe):
            pe.sem_inc(y_ready, CREDIT)
            pe.sem_inc(pv_done, PBUFS)
            pe.sem_inc(ot_ready, TURNED)
            pe.wait_ge(ident_ld, 16)
            pe.wait_ge(const_ld, 3 * 16)
            nc.tensor.transpose(ps[:, 2, 0:3 * E], wqkv_sb[:], ident[0:3 * E, 0:3 * E]).then_inc(wqkv_ps, 1)
            for c in range(NC):
                if c >= 2:
                    pe.wait_ge(xt_ready, c - 1)
                for k in range(4):
                    pe.wait_ge(xn_ready, 4 * c + k + 1)
                    ins = nc.tensor.transpose(ps[:, c % 2, P * k:P * k + P], xn[:, 4 * c + k, :], ident[:])
                ins.then_inc(xt_ps, 1)
            pe.wait_ge(wqkv_ready, 1)
            pe.wait_ge(xt_ready, NC)
            for t in range(NT):
                ins = nc.tensor.matmul(ps[:, 3, 3 * E * t:3 * E * t + 3 * E], xnT[:, P * t:P * t + P], wqkvT[:], start=True, stop=True)
            ins.then_inc(mix_ps, 1)
            pe.wait_ge(wmat_ld, 4 * 16)
            pe.wait_ge(wrap_ready, 1)
            for t in range(NT):
                if t % 4 == 0 and t >= 8:
                    pe.wait_ge(v_ready, t // 4 - 1)
                for ahead in range(2):
                    ins = nc.tensor.matmul(ps[:, 6 + t // 4 % 2, DM * (t % 4):DM * (t % 4) + DM],
                                           xnT[:, P * t + ahead:P * t + ahead + P], wmat[:, 2, :], start=ahead == 0, stop=ahead == 1)
                if t % 4 == 3:
                    ins.then_inc(v_ps, 1)

            def expert_weights(e, par):
                pe.wait_ge(w_ld[par], (e - par) * 40 + 80)
                for b in range(NF):
                    bank = 6 + (NF * par + b) % 2
                    pe.wait_ge(wT_ready, e * NF + b - 1 + CREDIT)
                    for f, (f0, n) in enumerate(FCH):
                        if b < 2:
                            ins = nc.tensor.transpose(ps[:, bank, f0:f0 + n], w1raw[0:n, par, NF * b + f, :], ident[0:n, 0:n])
                        else:
                            ins = nc.tensor.transpose(ps[0:n, bank, DM * f:DM * f + DM], w2raw[:, par, f0:f0 + n], ident[:])
                    ins.then_inc(tr_ready, 1)

            pe.wait_ge(v_ready, 4)
            expert_weights(0, 0)
            for n in range(16):
                i, c = n // NC, n % NC
                g, which = i // 2, i % 2
                if n >= 2:
                    pe.wait_ge(rot_ready, n - 1)
                for half in range(2):
                    ins = nc.tensor.matmul(ps[64 * half:64 * half + 64, 4 + n % 2, :], wmat[:, which, 64 * g:64 * g + 64],
                                           xnT[:, CW * c:CW * c + CW], start=True, stop=True, tile_position=(0, 64 * half))
                ins.then_inc(proj_ps, 1)
            pe.wait_ge(rot_ready, 16)

            def expert_out(e, par, c):
                n = e * NC + c
                pe.wait_ge(hid_ready, n * NF + NF + CREDIT)
                pe.wait_ge(y_added, n - 1 + ADDED)
                for k in range(4):
                    for f, (f0, rows) in enumerate(FCH):
                        ins = nc.tensor.matmul(ps[:, 4 + c % 2, DM * k:DM * k + DM], hid[0:rows, c % 2, f, P * k:P * k + P],
                                               w2T[0:rows, par, f, :], start=f == 0, stop=f == NF - 1)
                ins.then_inc(y_ready, 1)

            def expert(e, par, last):
                pe.wait_ge(wT_ready, e * NF + NF + CREDIT)
                for c in range(NC):
                    for f, (f0, rows) in enumerate(FCH):
                        k = c * NF + f
                        n = e * (NC * NF) + k
                        pe.wait_ge(silu_ready, n - 1 + CREDIT)
                        pe.wait_ge(hid_ready, n - 1 + CREDIT)
                        for b, ready in ((0, a_ready), (1, g_ready)):
                            nc.tensor.matmul(ps[0:rows, 2 * b + k % 2, :], w1T[:, par, F * b + f0:F * b + f0 + rows],
                                             xnT[:, CW * c:CW * c + CW], start=True, stop=True).then_inc(ready, 1)
                        if f == 0 and c > 0:
                            expert_out(e, par, c - 1)
                if not last:
                    expert_weights(e + 1, 1 - par)
                expert_out(e, par, NC - 1)

            with pe.Fori(0, E // 2 - 1) as pr:
                for par in range(2):
                    expert(pr * 2 + par, par, False)

            pe.wait_ge(wT_ready, (E - 1) * NF + CREDIT)
            pe.wait_ge(norm_parts, 5)
            pe.wait_ge(kmean_ready, 2)
            for t in range(NT):
                for i in range(4):
                    at = (i % 2) * NT * H + t * H + (i // 2) * 8
                    nc.tensor.matmul(ps[:, 7, at:at + 8], squares[i][:, P * t:P * t + P], sel16[:, 0, :], start=True, stop=True)
                for g in range(2):
                    at = t * H + g * 8
                    ins = nc.tensor.matmul(ps[:, 6, at:at + 8], parts[:, 2 * g, 0, P * t:P * t + P], sel16[:, 1 + g, :], start=True, stop=True)
            ins.then_inc(norms_ps, 1)
            pe.wait_ge(kmax_in, 1)
            nc.tensor.transpose(ps[0:H, 6, 256:256 + P], knorm[:, 0, :], ident[:]).then_inc(kmaxT_ps, 1)
            pe.wait_ge(kdiag_ready, 1)
            nc.tensor.matmul(ps[:, 6, 384:384 + H], ones[0:H, :], kdiag[:, 0, :], start=True, stop=True).then_inc(kmax_ps, 1)
            pe.wait_ge(use_ready, 1)
            nc.tensor.matmul(ps[0:1, 6, 400:400 + H], ones[:, 0:1], use_max[:], start=True, stop=True).then_inc(use_ps, 1)
            pe.wait_ge(flags_ready, 1)

            expert(E - 2, 0, False)
            expert(E - 1, 1, True)
            pe.wait_ge(hid_ready, E * NC * NF + CREDIT)
            pe.wait_ge(y_added, E * NC + ADDED)

            def scores(h, par, s, skipped):
                g = h * STEPS + s
                u, k = s // 8, s % 8
                if k == 0:
                    pe.wait_ge(shift_ld, (h * 2 + u + 1) * 32)
                for b in range(2):
                    t = 2 * k + b
                    pe.wait_ge(exp_done, g * 2 + b - 1 + CREDIT)
                    for c in range(2):
                        col = CW * (2 * u + c)
                        ins = nc.tensor.matmul(ps[:, SCORE_BANKS + 2 * b + c, :], ka[par][:, P * t:P * t + P],
                                               qa[par][:, col:col + CW], start=True, stop=True)
                        if skipped and b == 0 and c == 0:
                            ins.then_inc(m_ready, skipped)
                    ins.then_inc(score_ready, 1)
                    yield

            def max_scores(h, par, i):
                for c in range(NC):
                    m = (h * NT + i) * NC + c
                    pe.wait_ge(m_reduced, m - 1 + CREDIT)
                    nc.tensor.matmul(ps[:, M_BANK + c % 2, :], qa[par][0:KQ, P * i:P * i + P],
                                     ka[par][0:KQ, CW * c:CW * c + CW], start=True, stop=True).then_inc(m_ready, 1)
                    yield

            def weighted_values(h, par, s):
                g = h * STEPS + s
                u, k = s // 8, s % 8
                if s == 0:
                    pe.wait_ge(vh_ready, h + 1)
                if k == 0:
                    pe.wait_ge(o_copied, h * 2 + u)
                pe.wait_ge(exp_done, g * 2 + 2 + CREDIT)
                for b in range(2):
                    for c in range(2):
                        col = 32 * (2 * b + c)
                        ins = nc.tensor.matmul(ps[col:col + 32, O_BANK, :], vh[:, par, 2 * k + b, :], probs[:, s % PBUFS, b, c, :],
                                               start=k == 0, stop=k == 7, tile_position=(0, col))
                ins.then_inc(pv_done, 1)

            def turn_max(h, half):
                pe.wait_ge(mx_ready, h * 2 + half + 1)
                if not (isinstance(h, int) and h == 0 and half == 0):
                    pe.wait_ge(sum_ready, h * 2 + half - 1 + TURNED)
                nc.tensor.transpose(ps[0:8, T_BANK, 0:P], mx[:, half, :], ident[:]).then_inc(mxT_ready, 1)

            def turn_out(h, u):
                unit = h * 2 + u
                pe.wait_ge(o_copied, unit + 1)
                pe.wait_ge(shift_ready, unit + 1)
                pe.wait_ge(sum_ready, unit + TURNED)
                for b in range(4):
                    ins = nc.tensor.transpose(ps[:, T_BANK, P * b:P * b + P], osb[:, P * b:P * b + P], ident[:])
                ins.then_inc(ot_ready, 1)

            def all_of(gen):
                for _ in gen:
                    pass

            pe.wait_ge(aug_ld, 12 * 16)
            pe.wait_ge(ones_ready, 5)
            need = pe.value_load(flags[0:1, 0:1], min_val=0, max_val=P)
            with pe.If(need != 0):
                for i in range(LEAD):
                    all_of(max_scores(0, 0, i))
            with pe.Else():
                pe.sem_inc(m_ready, LEAD * NC)
            turn_max(0, 0)

            def step(h, par, s, first, last, with_max, skipped=0):
                if s == 4 and not last:
                    pe.wait_ge(aug_ld, h * 192 + 384)
                sc = scores(h, par, s, skipped)
                ms = iter(())
                if with_max:
                    ms = max_scores(h, par, s + LEAD) if s < 4 else max_scores(h + 1, 1 - par, s - 4)
                all_of(sc)
                next(ms, None)
                next(ms, None)
                if s >= PV_LAG:
                    weighted_values(h, par, s - PV_LAG)
                elif not first:
                    weighted_values(h - 1, 1 - par, s - PV_LAG + STEPS)
                all_of(ms)
                if s == 2 and not first:
                    turn_out(h - 1, 1)
                if s == 10:
                    turn_out(h, 0)
                if s == 5:
                    turn_max(h, 1)
                if s == 13 and not last:
                    turn_max(h + 1, 0)

            flag = [need]

            def run(part, steps, first, last):
                h = steps[0][0]
                if part == "b" and not last:
                    flag[0] = pe.value_load(flags[0:1, bass.ds(h + 1, 1)], min_val=0, max_val=P)
                if part == "b" and last:
                    for h, par, t in steps:
                        step(h, par, t, first, last, False)
                    return
                with pe.If(flag[0] != 0):
                    for h, par, t in steps:
                        step(h, par, t, first, last, True)
                with pe.Else():
                    for n, (h, par, t) in enumerate(steps):
                        step(h, par, t, first, last, False, len(steps) * NC if n == 0 else 0)

            run_heads(pe, run)
            for s in range(STEPS - PV_LAG, STEPS):
                weighted_values(H - 1, 1, s)
            turn_out(H - 1, 1)
            pe.wait_ge(attn_ready, 2 * H + TURNED)
            pe.wait_ge(wo_ready, 1)
            for q in range(4):
                for k in range(4):
                    ins = nc.tensor.transpose(ps[:, q, P * k:P * k + P], attn[:, 4 * q + k, :], ident[:])
                ins.then_inc(at_ps, 1)
            for q in range(4):
                pe.wait_ge(at_ready, q + 1)
                for k in range(4):
                    t = 4 * q + k
                    ins = nc.tensor.matmul(ps[:, 4 + q, DM * k:DM * k + DM], attnT[:, P * t:P * t + P], wo_mod[:], start=True, stop=True)
                ins.then_inc(fin_ps, 1)


_INS = ["L0_attn_x", "L0_attn_Wq", "L0_attn_Wk", "L0_attn_Wv", "L0_attn_Wo", "L0_attn_quantum_phase",
        "L0_attn_quantum_amplitude", "L0_ffn_wqkv", "L0_ffn_w1", "L0_ffn_w2"]


def kernel(**inputs):
    import concourse.bacc as _bacc
    from concourse.bass_utils import run_bass_kernel_spmd as _run

    angle = 2.0 * np.pi * np.arange(S, dtype=np.float64) / S
    rows = np.stack([np.cos(angle), np.sin(angle)]).astype(np.float32)
    shape_constants = {
        "identity": np.eye(P, dtype=np.float32),
        "descending": np.tile(np.arange(E, 0, -1, dtype=np.float32), (P, 1)),
        "cos_sin": np.repeat(rows, P // 2, axis=0),
        "head_of_row": np.tile(np.repeat(np.eye(8, dtype=np.float32), D, axis=0), (2, 1)),
    }
    nc = _bacc.Bacc("TRN2", target_bir_lowering=False, num_devices=1)
    arrays, args = {}, []
    for name in _INS:
        arrays[f"in_{name}"] = np.ascontiguousarray(inputs[name])
    arrays.update(shape_constants)
    for name, a in arrays.items():
        args.append(nc.dram_tensor(name, a.shape, mybir.dt.from_np(a.dtype), kind="ExternalInput").ap())
    out = nc.dram_tensor("out", (1, S, DM), F32, kind="ExternalOutput").ap()
    build(nc, *args, out)
    result = _run(nc, [arrays], core_ids=[0])
    return result.results[0]["out"]
```

```python
from contextlib import ExitStack

import numpy as np

import concourse.bass as bass
from concourse import mybir

F32 = mybir.dt.float32
BF16 = mybir.dt.bfloat16
ALU = mybir.AluOpType
ACT = mybir.ActivationFunctionType
AX = mybir.AxisListType.X

P = 128
S = 2048
DM = 128
H = 16
D = 8
E = 8
F = 352
NT = S // P
CW = 512
NC = S // CW
FCH = [(0, 128), (128, 128), (256, 96)]
NF = len(FCH)
MAX_TILES = (2 * S + E * (P - 1)) // P
GROUP = 4
TILES = -(-MAX_TILES // GROUP) * GROUP
FP = NF * P
ROWS = 2 * D
KQ = 6 * ROWS
KS = KQ + 2
STEPS = NT
CREDIT = 2
PBUFS = 4
PV_LAG = 2
TURNED = 1
ISQ8 = float(1.0 / np.sqrt(D))
TWO_PI = 2.0 * np.pi
PI_A = 6.28125
PI_B = float(np.float32(2.0 ** -20 * np.floor((TWO_PI - PI_A) * 2.0 ** 20)))
PI_C = float(TWO_PI - PI_A - PI_B)
ROUND = 12582912.0
PI_DOWN = 3.1415925
LOWEST = -3.0e38
EPS = 1e-5
SCORE_BANKS, O_BANK, T_BANK, M_BANK = 0, 4, 5, 6
SPAN, BELOW = 130.0, 62.0
SQ8 = float(np.sqrt(D))
SLACK = 1.02
ONES = 5
LEAD = 12


def build(nc, x, Wq, Wk, Wv, Wo, phase, amp, wqkv, w1, w2, ident_in, desc_in, cs_in, sel_in, tri_in, below_in, count_in, out):
    scratch = nc.dram_tensor("qk_parts", [2, 3, H, ROWS, S], BF16, kind="Internal").ap()
    slots_x = nc.dram_tensor("slots_x", [TILES * P, DM], F32, kind="Internal").ap()
    slots_y = nc.dram_tensor("slots_y", [TILES * P, DM], F32, kind="Internal").ap()
    tiles_x = slots_x.rearrange("(n p) d -> p n d", p=P)
    tiles_y = slots_y.rearrange("(n p) d -> p n d", p=P)
    x_v = x.rearrange("a (t p) d -> p (a t) d", p=P)
    out_v = out.rearrange("a (t p) d -> p (a t) d", p=P)

    with ExitStack() as ctx:
        def sb(name, shape, dt):
            return ctx.enter_context(nc.sbuf_tensor(name, shape, dt))

        def sem(name):
            return ctx.enter_context(nc.semaphore(name))

        acc = sb("acc", [P, NT, DM], F32)
        xnT = sb("xnT", [P, S + 1], F32)
        big = sb("big", [P, 4, S], F32)
        rotated = [big[:, i, :] for i in range(4)]
        probs = big[:].rearrange("p a (b c n) -> p a b c n", b=2, c=2)
        parts = sb("parts", [P, 4, 3, S], BF16)
        attn = parts[:, 1, 0:2, :].rearrange("p a n -> p (a n)").bitcast(F32).rearrange("p (t d) -> p t d", d=DM)
        parts_f32 = parts[:].rearrange("p a b n -> p (a b n)").bitcast(F32)
        w1raw = parts_f32[:, 0:E * 2 * NF * DM].rearrange("p (b e h) -> p b e h", b=2 * NF, h=DM)
        w2raw = parts_f32[:, E * 2 * NF * DM:E * (2 * NF * DM + F)].rearrange("p (e f) -> p e f", f=F)
        gathered = parts[:, 2:4, :, :].rearrange("p a b n -> p (a b n)").bitcast(F32)[:, 0:2 * NT * DM].rearrange(
            "p (r t d) -> p r t d", r=2, d=DM)
        cs = sb("cs", [P, S], F32)
        hid = cs[:, 0:2 * FP].rearrange("p (a f) -> p a f", a=2)
        hidT = cs[:, 2 * FP:4 * FP].rearrange("p (a f s) -> p a f s", a=2, f=NF)
        xg = cs[:, 4 * FP:4 * FP + 4 * DM].rearrange("p (a d) -> p a d", a=4)
        ident = sb("ident", [P, P], F32)
        desc = sb("desc", [P, E], F32)
        sel = sb("sel", [P, 8], F32)
        sel16 = sb("sel16", [P, 3, 8], BF16)
        squares = [big[:, i, 0:S // 2].bitcast(BF16) for i in range(4)]
        kmean = sb("kmean", [P, 2], F32)
        ones = sb("ones", [P, P], F32)
        knorm = sb("knorm", [P, 2, H], F32)
        kdiag = sb("kdiag", [H, 2, H], F32)
        bound = sb("bound", [P, 3, NT, H], F32)
        use_max = sb("use_max", [P, H], F32)
        flags = sb("flags", [1, H], mybir.dt.int32)
        other = sb("other", [P, H, NT], F32)
        wmat = sb("wmat", [P, 4, DM], F32)
        wo_mod = sb("wo_mod", [P, DM], F32)
        wqkv_sb = sb("wqkv_sb", [3 * E, DM], F32)
        wqkvT = sb("wqkvT", [P, 3 * E], F32)
        stats = sb("stats", [P, NT, 6], F32)
        mv = sb("mv", [P, NT, 2], F32)
        ve = sb("ve", [P, 4, NT], F32)
        rstd = sb("rstd", [P, NT], F32)
        ang = sb("ang", [P, 8, 3], F32)
        mod = sb("mod", [P, 3], F32)
        mix = sb("mix", [P, NT, 3 * E], F32)
        pair = sb("pair", [P, NT, E, E], F32)
        gate = sb("gate", [P, 8, NT, E], F32)
        top = sb("top", [P, 8, NT], F32)
        chosen = sb("chosen", [P, NT + 1, E], F32)
        slot_of = sb("slot_of", [P, NT, E], F32)
        tri = sb("tri", [P, P], F32)
        below = sb("below", [P, E, E], F32)
        count = sb("count", [1, TILES, E], F32)
        tiles_of = sb("tiles_of", [P, 6, E], F32)
        before = sb("before", [P, E, E], F32)
        ended = sb("ended", [1, TILES, E], F32)
        owner = sb("owner", [1, 2, TILES], F32)
        expert_of = sb("expert_of", [1, TILES], mybir.dt.int32)
        slot_f = sb("slot_f", [P, 2, NT], F32)
        slot = sb("slot", [P, 2, NT], mybir.dt.uint32)
        w1T = sb("w1T", [P, E, 2 * F], F32)
        w2T = sb("w2T", [P, E, NF, DM], F32)
        silu = pair[:].rearrange("p t e j -> p (t e j)")[:, 0:2 * F].rearrange("p (a f) -> p a f", a=2)
        xgT = sb("xgT", [P, 2, P], F32)
        y = sb("y", [P, 4, DM], F32)
        vaug = sb("vaug", [P, H, NT, D + 1], F32)
        vh = sb("vh", [P, 2, NT, 32], F32)
        qa = [sb(f"qa{i}", [KS, S], BF16) for i in range(2)]
        ka = [sb(f"ka{i}", [KS, S], BF16) for i in range(2)]
        m4 = sb("m4", [P, NT, NC], F32)
        mx = sb("mx", [P, 2, 8], F32)
        shift = sb("shift", [8, 2, P], BF16)
        osb = sb("osb", [P, CW], F32)
        half_sum = sb("half_sum", [P, 4, 2, D + 1], F32)
        sums = sb("sums", [P, 4, 2, D + 1], F32)
        rden = sb("rden", [P, 4, 2, 1], F32)
        attnT = sb("attnT", [P, S], F32)
        xn = attnT[:].rearrange("p (t d) -> p t d", d=DM)
        ps = ctx.enter_context(nc.psum_tensor("ps", [P, 8, CW], F32))

        x_in = [sem(f"x_in{i}") for i in range(4)]
        ident_ld, const_ld, wmat_ld, phase_ld, cs_ld = (sem(n) for n in ("ident_ld", "const_ld", "wmat_ld", "phase_ld", "cs_ld"))
        w_ld, route_ld = sem("w_ld"), sem("route_ld")
        dve_step, var_ready, sd_ready, xn_ready = (sem(n) for n in ("dve_step", "var_ready", "sd_ready", "xn_ready"))
        xt_ps, xt_ready, wrap_ready = (sem(n) for n in ("xt_ps", "xt_ready", "wrap_ready"))
        ang_ready, sin_ready, mod_ready = (sem(n) for n in ("ang_ready", "sin_ready", "mod_ready"))
        wqkv_ps, wqkv_ready, mix_ps = (sem(n) for n in ("wqkv_ps", "wqkv_ready", "mix_ps"))
        gexp_in, gexp_out = (sem(n) for n in ("gexp_in", "gexp_out"))
        chosen_ready, rank_ps, slot_ready, owner_ready, zeros_wr, scattered = (
            sem(n) for n in ("chosen_ready", "rank_ps", "slot_ready", "owner_ready", "zeros_wr", "scattered"))
        norm_parts, kmean_ready = sem("norm_parts"), sem("kmean_ready")
        proj_ps, rot_ready, v_ps, v_ready, ones_ready = (sem(n) for n in ("proj_ps", "rot_ready", "v_ps", "v_ready", "ones_ready"))
        hi_ready, rest1_ready, mid_ready, rest2_ready, parts_ready, scratch_wr = (
            sem(n) for n in ("hi_ready", "rest1_ready", "mid_ready", "rest2_ready", "parts_ready", "scratch_wr"))
        norms_ps, kmax_in, kmaxT_ps, kdiag_ready, kmax_ps, use_ready, use_ps, flags_ready = (
            sem(n) for n in ("norms_ps", "kmax_in", "kmaxT_ps", "kdiag_ready", "kmax_ps", "use_ready", "use_ps", "flags_ready"))
        tr_ready, wT_ready = sem("tr_ready"), sem("wT_ready")
        xg_ld, y_wr = ([sem(f"{n}{half}") for half in range(2)] for n in ("xg_ld", "y_wr"))
        xgT_ps, xgT_ready, a_ready, g_ready, silu_ready = (
            sem(n) for n in ("xgT_ps", "xgT_ready", "a_ready", "g_ready", "silu_ready"))
        pad_ready, hid_ready, hidT_ps, hidT_ready, y_ready, y_copied, gather_ld, y_added = (
            sem(n) for n in ("pad_ready", "hid_ready", "hidT_ps", "hidT_ready", "y_ready", "y_copied", "gather_ld", "y_added"))
        aug_ld, score_ready, exp_done, pv_done, vh_ready = (
            sem(n) for n in ("aug_ld", "score_ready", "exp_done", "pv_done", "vh_ready"))
        m_ready, m_reduced, mx_ready, mxT_ready, shift_hi, shift_ready, shift_ld = (
            sem(n) for n in ("m_ready", "m_reduced", "mx_ready", "mxT_ready", "shift_hi", "shift_ready", "shift_ld"))
        o_copied, ot_ready, half_ready, sum_ready, rden_ready, attn_ready = (
            sem(n) for n in ("o_copied", "ot_ready", "half_ready", "sum_ready", "rden_ready", "attn_ready"))
        at_ps, at_ready, fin_ps, fin_ready, out_wr, wo_ready = (
            sem(n) for n in ("at_ps", "at_ready", "fin_ps", "fin_ready", "out_wr", "wo_ready"))

        block = ctx.enter_context(nc.Block())

        def after(eng, signal, value):
            if not (isinstance(value, int) and value <= 0):
                eng.wait_ge(signal, value)

        def run_tiles(eng, tile):
            for k in range(GROUP):
                tile(k, k, False)
            with eng.Fori(1, TILES // GROUP - 1) as g:
                for k in range(GROUP):
                    tile(g * GROUP + k, k, False)
            for k in range(GROUP):
                tile(TILES - GROUP + k, k, k == GROUP - 1)

        def part_a(h, par):
            return [(h, par, t) for t in range(NT - LEAD)]

        def part_b(h, par):
            return [(h, par, t) for t in range(NT - LEAD, STEPS)]

        def run_heads(eng, run):
            run("a", part_a(0, 0), True, False)
            with eng.Fori(0, H // 2 - 1) as pr:
                for par in range(2):
                    run("b", part_b(pr * 2 + par, par), False, False)
                    run("a", part_a(pr * 2 + par + 1, 1 - par), False, False)
            run("b", part_b(H - 2, 0), False, False)
            run("a", part_a(H - 1, 1), False, True)
            run("b", part_b(H - 1, 1), False, True)

        def run_steps(eng, step):
            def run(part, steps, first, last):
                for h, par, t in steps:
                    step(h, par, t, first, last)
            run_heads(eng, run)

        @block.sync
        def _(sp):
            for i in range(4):
                sp.dma_start(acc[:, 4 * i:4 * i + 4, :], x_v[:, 4 * i:4 * i + 4, :]).then_inc(x_in[i], 16)
            sp.dma_start(ident[:], ident_in).then_inc(ident_ld, 16)
            sp.dma_start(desc[:], desc_in).then_inc(const_ld, 16)
            sp.dma_start(sel[:], sel_in).then_inc(const_ld, 16)
            sp.dma_start(wqkv_sb[:], wqkv).then_inc(const_ld, 16)
            for i, w in enumerate((Wq, Wk, Wv, Wo)):
                sp.dma_start(wmat[:, i, :], w).then_inc(wmat_ld, 16)
            for src, at in ((phase, 0), (amp, 1)):
                for g in range(2):
                    for half in range(2):
                        sp.dma_start(ang[64 * half:64 * half + 64, at, g:g + 1],
                                     src[8 * g:8 * g + 8, :].rearrange("h (d o) -> (h d) o", o=1)).then_inc(phase_ld, 16)
                sp.dma_start(ang[:, at, 2:3], src.rearrange("h (d o) -> (h d) o", o=1)).then_inc(phase_ld, 16)

            for b in range(2):
                for f, (f0, rows) in enumerate(FCH):
                    sp.dma_start(w1raw[0:rows, NF * b + f, :, :],
                                 w1[:, F * b + f0:F * b + f0 + rows, :].rearrange("e p h -> p e h")).then_inc(w_ld, 16)
            sp.dma_start(w2raw, w2.rearrange("e p f -> p e f")).then_inc(w_ld, 16)
            for dst, src in ((tri, tri_in), (below, below_in), (count, count_in)):
                sp.dma_start(dst[:], src).then_inc(route_ld, 16)
            sp.dma_start(cs[:], cs_in).then_inc(cs_ld, 16)
            sp.wait_ge(ones_ready, ONES)
            for i in range(0, TILES, 8):
                sp.dma_start(tiles_x[:, i:i + 8, :], vh[:].rearrange("p a t d -> p (a t d)")
                             .rearrange("p (n d) -> p n d", d=DM)).then_inc(zeros_wr, 16)

            for i in range(4):
                sp.wait_ge(parts_ready, i + 1)
                g, which = i // 2, i % 2
                for part in range(3):
                    for half in range(2):
                        sp.dma_start(scratch[which, part, 8 * g:8 * g + 8, 8 * half:8 * half + 8, :],
                                     parts[64 * half:64 * half + 64, i, part, :]).then_inc(scratch_wr, 16)
            sp.wait_ge(scratch_wr, 24 * 16)

            def load_head(h, par):
                q_parts, k_parts = (0, 0, 0, 1, 1, 2), (0, 1, 2, 0, 1, 0)
                for buf, which, order in ((qa[par], 0, q_parts), (ka[par], 1, k_parts)):
                    for b, part in enumerate(order):
                        sp.dma_start(buf[ROWS * b:ROWS * b + ROWS, :], scratch[which, part, h, :, :]).then_inc(aug_ld, 16)

            def load_shift(h, par, half):
                sp.wait_ge(shift_ready, h * 2 + half + 1)
                for r in range(2):
                    sp.dma_start(qa[par][KQ + r:KQ + r + 1, 1024 * half:1024 * half + 1024].rearrange("o (t p) -> o t p", p=P),
                                 shift[:, r, :]).then_inc(shift_ld, 16)

            load_head(0, 0)

            def load_rows(m, half):
                after(sp, xgT_ps, m * 2 - 2)
                sp.dma_start(xg[:, 2 * half:2 * half + 2, :], tiles_x[:, bass.ds(m * 2, 2), :]).then_inc(xg_ld[half], 16)

            sp.wait_ge(scattered, 2 * NT * 16)
            load_rows(0, 0)
            load_rows(1, 1)
            with sp.Fori(1, TILES // 4) as g:
                for half in range(2):
                    load_rows(g * 2 + half, half)
            load_shift(0, 0, 0)

            def step(h, par, s, first, last):
                if s == 0 and not last:
                    sp.wait_ge(score_ready, h * (2 * STEPS))
                    load_head(h + 1, 1 - par)
                if s == 5:
                    load_shift(h, par, 1)
                if s == 13 and not last:
                    load_shift(h + 1, 1 - par, 0)

            run_steps(sp, step)
            for q in range(4):
                sp.wait_ge(fin_ready, q + 1)
                sp.dma_start(out_v[:, 4 * q:4 * q + 4, :], acc[:, 4 * q:4 * q + 4, :]).then_inc(out_wr, 16)
            sp.wait_ge(out_wr, 4 * 16)

        @block.gpsimd
        def _(pool):
            nc.gpsimd.memset(vaug[:], 1.0).then_inc(ones_ready, 1)
            nc.gpsimd.memset(vh[:], 0.0).then_inc(ones_ready, 1)
            pool.wait_ge(const_ld, 3 * 16)
            nc.gpsimd.tensor_copy(sel16[:, 0, :], sel[:]).then_inc(norm_parts, 1)

            def head_values(h, par):
                nc.gpsimd.tensor_copy(vh[:, par, :, 0:D + 1], vaug[:, bass.ds(h, 1), :, :].rearrange("p o t d -> p (o t) d")).then_inc(vh_ready, 1)

            pool.wait_ge(v_ready, 4)
            pool.wait_ge(ones_ready, ONES)
            pool.wait_ge(zeros_wr, TILES // 8 * 16)
            head_values(0, 0)

            pool.wait_ge(xn_ready, NT)
            pool.wait_ge(slot_ready, 1)
            for r in range(2):
                for t in range(NT):
                    nc.gpsimd.indirect_dma_start(slots_x, bass.IndirectOffsetOnAxis(ap=slot[:, r, t:t + 1], axis=0),
                                                 xn[:, t, :], None).then_inc(scattered, 16)

            def store_results(m, half):
                pool.wait_ge(y_copied, m * 2 + 2)
                nc.gpsimd.dma_start(tiles_y[:, bass.ds(m * 2, 2), :], y[:, 2 * half:2 * half + 2, :]).then_inc(y_wr[half], 16)

            with pool.Fori(0, TILES // 4) as g:
                for half in range(2):
                    store_results(g * 2 + half, half)

            def gather_results():
                for half in range(2):
                    pool.wait_ge(y_wr[half], TILES // 4 * 16)
                pool.wait_ge(scratch_wr, 24 * 16)
                for r in range(2):
                    for t in range(NT):
                        nc.gpsimd.indirect_dma_start(gathered[:, r, t, :], None, slots_y,
                                                     bass.IndirectOffsetOnAxis(ap=slot[:, r, t:t + 1], axis=0)).then_inc(gather_ld, 16)

            def step(h, par, s, first, last):
                if s == 1 and not last:
                    pool.wait_ge(pv_done, h * STEPS + PBUFS)
                    head_values(h + 1, 1 - par)

            def run(part, steps, first, last):
                for h, par, t in steps:
                    step(h, par, t, first, last)
                if first:
                    gather_results()

            run_heads(pool, run)

        @block.scalar
        def _(act):
            act.sem_inc(wT_ready, CREDIT)
            act.sem_inc(exp_done, CREDIT)
            act.wait_ge(var_ready, 1)
            nc.scalar.activation(ve[:, 1, :], ve[:, 0, :], ACT.Sqrt).then_inc(sd_ready, 1)
            act.wait_ge(ang_ready, 1)
            nc.scalar.activation(ang[:, 5, :], ang[:, 4, :], ACT.Sin, scale=0.5).then_inc(sin_ready, 1)
            act.wait_ge(wqkv_ps, 1)
            nc.scalar.copy(wqkvT[:], ps[:, 2, 0:3 * E]).then_inc(wqkv_ready, 1)
            for c in range(NC):
                act.wait_ge(xt_ps, c + 1)
                nc.scalar.copy(xnT[:, CW * c:CW * c + CW], ps[:, c % 2, :]).then_inc(xt_ready, 1)
            act.wait_ge(xt_ready, 1)
            nc.scalar.copy(xnT[:, S:S + 1], xnT[:, 0:1]).then_inc(wrap_ready, 1)
            act.wait_ge(ones_ready, ONES)
            for q in range(4):
                act.wait_ge(v_ps, q + 1)
                nc.scalar.copy(vaug[:, :, 4 * q:4 * q + 4, 0:D],
                               ps[:, 6 + q % 2, :].rearrange("p (t h d) -> p h t d", t=4, h=H)).then_inc(v_ready, 1)

            def expert_weights(e):
                for b in range(NF):
                    act.wait_ge(tr_ready, e * NF + b + 1)
                    bank = 6 + (e * NF + b) % 2
                    if b < 2:
                        nc.scalar.copy(w1T[:, e, F * b:F * b + F], ps[:, bank, 0:F]).then_inc(wT_ready, 1)
                    else:
                        nc.scalar.copy(w2T[:, e, 0:2, :], ps[:, bank, 0:2 * DM].rearrange("p (c h) -> p c h", h=DM))
                        nc.scalar.copy(w2T[0:96, e, 2, :], ps[0:96, bank, 2 * DM:3 * DM]).then_inc(wT_ready, 1)

            for r in range(2):
                act.wait_ge(gexp_in, r + 1)
                if r == 0:
                    nc.scalar.activation(pair[:], pair[:], ACT.Exp).then_inc(gexp_out, 1)
                    for e in range(E // 2):
                        expert_weights(e)
                else:
                    nc.scalar.activation(top[:, 5, :], top[:, 4, :], ACT.Exp).then_inc(gexp_out, 1)

            for e in range(E // 2, E):
                expert_weights(e)

            def part_of(i, part):
                ready, done = ((rot_ready, hi_ready), (rest1_ready, mid_ready), (rest2_ready, parts_ready))[part]
                act.wait_ge(ready, 4 * (i + 1) if part == 0 else i + 1)
                act.wait_ge(tr_ready, E * NF)
                nc.scalar.copy(parts[:, i, part, :], rotated[i]).then_inc(done, 1)

            part_of(0, 0)
            for i in range(4):
                part_of(i, 1)
                if i < 3:
                    part_of(i + 1, 0)
                part_of(i, 2)

            def rows_out(n, k):
                act.wait_ge(xgT_ps, n + 1)
                after(act, g_ready, n - 1)
                nc.scalar.copy(xgT[:, k % 2, :], ps[:, 4, 0:P]).then_inc(xgT_ready, 1)

            def results_out(n, k):
                act.wait_ge(y_ready, n + 1)
                after(act, y_wr[k // 2 % 2], (n - k % 4) * 4)
                nc.scalar.copy(y[:, k % 4, :], ps[:, 5, 0:DM]).then_inc(y_copied, 1)

            def tile(n, k, last):
                act.wait_ge(a_ready, n + 1)
                after(act, hid_ready, n - 1)
                nc.scalar.activation(silu[:, k % 2, :], ps[:, k % 2, 0:F], ACT.Silu).then_inc(silu_ready, 1)
                if not last:
                    rows_out(n + 1, k + 1)
                if not (isinstance(n, int) and n < 2):
                    results_out(n - 2, k + 2)

            rows_out(0, 0)
            run_tiles(act, tile)
            for n in range(TILES - 2, TILES):
                results_out(n, n)

            def copy_out(unit, steps_done):
                act.wait_ge(pv_done, steps_done + PBUFS)
                act.wait_ge(ot_ready, unit + TURNED)
                nc.scalar.copy(osb[:], ps[:, O_BANK, :]).then_inc(o_copied, 1)

            def step(h, par, s, first, last):
                g = h * STEPS + s
                for b in range(2):
                    act.wait_ge(score_ready, g * 2 + b + 1)
                    act.wait_ge(pv_done, g + 1)
                    nc.scalar.activation(probs[:, s % PBUFS, b, :, :], ps[:, 2 * b:2 * b + 2, :], ACT.Exp, scale=ISQ8).then_inc(exp_done, 1)
                if s == PV_LAG - 1 and not first:
                    copy_out(h * 2 - 1, h * STEPS)
                if s == 8 + PV_LAG - 1:
                    copy_out(h * 2, h * STEPS + 8)

            run_steps(act, step)
            copy_out(2 * H - 1, H * STEPS)
            for q in range(4):
                act.wait_ge(at_ps, q + 1)
                nc.scalar.copy(attnT[:, CW * q:CW * q + CW], ps[:, q, :]).then_inc(at_ready, 1)

        @block.vector
        def _(dve):
            chain = [0]

            def then(ins):
                chain[0] += 1
                ins.then_inc(dve_step, 1)
                dve.wait_ge(dve_step, chain[0])

            dve.sem_inc(m_reduced, CREDIT)
            dve.sem_inc(sum_ready, TURNED)
            dve.sem_inc(attn_ready, TURNED)
            nc.vector.memset(ones[:], 1.0).then_inc(ones_ready, 1)
            for i in range(2):
                nc.vector.memset(ka[i][KQ:KS, :], 1.0).then_inc(ones_ready, 1)
            for t in range(NT):
                if t % 4 == 0:
                    dve.wait_ge(x_in[t // 4], 16)
                ins = nc.vector.bn_stats(stats[:, t, :], acc[:, t, :])
            then(ins)
            for t in range(NT):
                ins = nc.vector.bn_aggr(mv[:, t, :], stats[:, t, :])
            then(ins)
            nc.vector.tensor_scalar(ve[:, 0, :], mv[:, :, 1], EPS, None, ALU.add).then_inc(var_ready, 1)
            dve.wait_ge(sd_ready, 1)
            then(nc.vector.reciprocal(rstd[:], ve[:, 1, :]))
            then(nc.vector.tensor_tensor(ve[:, 2, :], rstd[:], rstd[:], ALU.mult))
            then(nc.vector.tensor_tensor(ve[:, 3, :], ve[:, 2, :], ve[:, 0, :], ALU.mult))
            then(nc.vector.tensor_scalar(ve[:, 2, :], ve[:, 3, :], -0.5, 1.5, ALU.mult, ALU.add))
            then(nc.vector.tensor_tensor(rstd[:], rstd[:], ve[:, 2, :], ALU.mult))
            for t in range(NT):
                nc.vector.tensor_scalar(xn[:, t, :], acc[:, t, :], mv[:, t, 0:1], rstd[:, t:t + 1],
                                        ALU.subtract, ALU.mult).then_inc(xn_ready, 1)
            dve.wait_ge(phase_ld, 10 * 16)
            then(nc.vector.tensor_scalar(ang[:, 2, :], ang[:, 0, :], float(1.0 / TWO_PI), ROUND, ALU.mult, ALU.add))
            then(nc.vector.tensor_scalar(ang[:, 3, :], ang[:, 2, :], ROUND, None, ALU.subtract))
            then(nc.vector.scalar_tensor_tensor(ang[:, 4, :], ang[:, 3, :], -PI_A, ang[:, 0, :], ALU.mult, ALU.add))
            then(nc.vector.scalar_tensor_tensor(ang[:, 6, :], ang[:, 3, :], -PI_B, ang[:, 4, :], ALU.mult, ALU.add))
            then(nc.vector.scalar_tensor_tensor(ang[:, 7, :], ang[:, 3, :], -PI_C, ang[:, 6, :], ALU.mult, ALU.add))
            nc.vector.tensor_scalar(ang[:, 4, :], ang[:, 7, :], PI_DOWN, -PI_DOWN, ALU.min, ALU.max).then_inc(ang_ready, 1)
            dve.wait_ge(sin_ready, 1)
            then(nc.vector.tensor_tensor(ang[:, 6, :], ang[:, 5, :], ang[:, 5, :], ALU.mult))
            then(nc.vector.tensor_scalar(ang[:, 7, :], ang[:, 6, :], -2.0, 1.0, ALU.mult, ALU.add))
            then(nc.vector.tensor_tensor(mod[:], ang[:, 7, :], ang[:, 1, :], ALU.mult))
            dve.wait_ge(wmat_ld, 4 * 16)
            nc.vector.tensor_scalar(wo_mod[:], wmat[:, 3, :], mod[:, 2:3], float(1.0 / np.sqrt(2.0)), ALU.mult, ALU.mult).then_inc(wo_ready, 1)

            def over_j(ap):
                return ap.unsqueeze(3).to_broadcast([P, NT, E, E])

            def over_e(ap):
                return ap.unsqueeze(2).to_broadcast([P, NT, E, E])

            def by_token(ap):
                return ap.unsqueeze(2).to_broadcast([P, NT, E])

            dve.wait_ge(mix_ps, 1)
            then(nc.vector.tensor_copy(mix[:], ps[:, 3, 0:NT * 3 * E].rearrange("p (t n) -> p t n", t=NT)))
            then(nc.vector.tensor_tensor(pair[:], over_j(mix[:, :, 0:E]), over_e(mix[:, :, E:2 * E]), ALU.mult))
            then(nc.vector.tensor_reduce(gate[:, 0, :, :], pair[:], AX, ALU.max))
            nc.vector.tensor_tensor(pair[:], pair[:], over_j(gate[:, 0, :, :]), ALU.subtract).then_inc(gexp_in, 1)
            dve.wait_ge(gexp_out, 1)
            then(nc.vector.tensor_reduce(gate[:, 1, :, :], pair[:], AX, ALU.add))
            then(nc.vector.tensor_tensor(pair[:], pair[:], over_e(mix[:, :, 2 * E:3 * E]), ALU.mult))
            then(nc.vector.tensor_reduce(gate[:, 2, :, :], pair[:], AX, ALU.add))
            then(nc.vector.reciprocal(gate[:, 3, :, :], gate[:, 1, :, :]))
            then(nc.vector.tensor_tensor(gate[:, 4, :, :], gate[:, 2, :, :], gate[:, 3, :, :], ALU.mult))
            dve.wait_ge(const_ld, 3 * 16)
            order = desc[:].unsqueeze(1).to_broadcast([P, NT, E])
            for r, (logits, mask) in enumerate(((4, 5), (6, 7))):
                then(nc.vector.tensor_reduce(top[:, r, :], gate[:, logits, :, :], AX, ALU.max))
                then(nc.vector.tensor_tensor(gate[:, 0, :, :], gate[:, logits, :, :], by_token(top[:, r, :]), ALU.is_equal))
                then(nc.vector.tensor_tensor(gate[:, 1, :, :], gate[:, 0, :, :], order, ALU.mult))
                then(nc.vector.tensor_reduce(top[:, 2 + r, :], gate[:, 1, :, :], AX, ALU.max))
                then(nc.vector.tensor_tensor(gate[:, mask, :, :], gate[:, 1, :, :], by_token(top[:, 2 + r, :]), ALU.is_equal))
                if r == 0:
                    then(nc.vector.scalar_tensor_tensor(gate[:, 6, :, :], gate[:, mask, :, :], LOWEST, gate[:, 4, :, :], ALU.mult, ALU.add))
            nc.vector.tensor_tensor(top[:, 4, :], top[:, 1, :], top[:, 0, :], ALU.subtract).then_inc(gexp_in, 1)
            nc.vector.tensor_tensor(chosen[:, 0:NT, :], gate[:, 5, :, :], gate[:, 7, :, :], ALU.add).then_inc(chosen_ready, 1)
            nc.vector.memset(chosen[:, NT, :], 0.0).then_inc(chosen_ready, 1)
            dve.wait_ge(gexp_out, 2)
            then(nc.vector.tensor_scalar(top[:, 6, :], top[:, 5, :], 1.0, None, ALU.add))
            then(nc.vector.reciprocal(top[:, 6, :], top[:, 6, :]))
            then(nc.vector.tensor_tensor(top[:, 7, :], top[:, 5, :], top[:, 6, :], ALU.mult))
            dve.wait_ge(rank_ps, 1)
            dve.wait_ge(route_ld, 3 * 16)
            rank = ps[:, 3, 0:NT * E].rearrange("p (t e) -> p t e", e=E)
            then(nc.vector.tensor_scalar(tiles_of[:, 0, :], ps[:, 3, NT * E:NT * E + E], 1.0 / P, 0.5 - 0.5 / P, ALU.mult, ALU.add))
            then(nc.vector.tensor_scalar(tiles_of[:, 1, :], tiles_of[:, 0, :], ROUND, None, ALU.add))
            then(nc.vector.tensor_scalar(tiles_of[:, 2, :], tiles_of[:, 1, :], ROUND, None, ALU.subtract))
            then(nc.vector.tensor_tensor(before[:], below[:], tiles_of[:, 2, :].unsqueeze(1).to_broadcast([P, E, E]), ALU.mult))
            then(nc.vector.tensor_reduce(tiles_of[:, 3, :], before[:], AX, ALU.add))
            then(nc.vector.tensor_scalar(tiles_of[:, 4, :], tiles_of[:, 3, :], float(P), None, ALU.mult))
            then(nc.vector.tensor_tensor(slot_of[:], rank, tiles_of[:, 4, :].unsqueeze(1).to_broadcast([P, NT, E]), ALU.add))
            for r, mask in enumerate((5, 7)):
                then(nc.vector.tensor_tensor(gate[:, r, :, :], slot_of[:], gate[:, mask, :, :], ALU.mult))
                then(nc.vector.tensor_reduce(slot_f[:, r, :], gate[:, r, :, :], AX, ALU.add))
            nc.vector.tensor_copy(slot[:], slot_f[:]).then_inc(slot_ready, 1)
            then(nc.vector.tensor_tensor(tiles_of[0:1, 5, :], tiles_of[0:1, 3, :], tiles_of[0:1, 2, :], ALU.add))
            then(nc.vector.tensor_tensor(ended[:], count[:], tiles_of[0:1, 5, :].unsqueeze(1).to_broadcast([1, TILES, E]), ALU.is_ge))
            then(nc.vector.tensor_reduce(owner[:, 0, :], ended[:], AX, ALU.add))
            then(nc.vector.tensor_scalar(owner[:, 1, :], owner[:, 0, :], float(E - 1), None, ALU.min))
            nc.vector.tensor_copy(expert_of[:], owner[:, 1, :]).then_inc(owner_ready, 1)
            dve.wait_ge(cs_ld, 16)

            def rest(i, part):
                dve.wait_ge((hi_ready, mid_ready)[part], i + 1)
                nc.vector.tensor_tensor(rotated[i], rotated[i], parts[:, i, part, :], ALU.subtract).then_inc((rest1_ready, rest2_ready)[part], 1)

            def square(i):
                dve.wait_ge(parts_ready, i + 1)
                nc.vector.tensor_tensor(squares[i], parts[:, i, 0, :], parts[:, i, 0, :], ALU.mult).then_inc(norm_parts, 1)

            for i in range(4):
                for c in range(NC):
                    n = i * NC + c
                    dve.wait_ge(proj_ps, n + 1)
                    nc.vector.scalar_tensor_tensor(rotated[i][:, CW * c:CW * c + CW], ps[:, 4 + n % 2, :], mod[:, i // 2:i // 2 + 1],
                                                   cs[:, CW * c:CW * c + CW], ALU.mult, ALU.mult).then_inc(rot_ready, 1)
                    if i > 0 and c == 1:
                        rest(i - 1, 0)
                    if i > 0 and c == 3:
                        rest(i - 1, 1)
                    if i > 1 and c == 0:
                        square(i - 2)
            rest(3, 0)
            square(2)
            rest(3, 1)
            square(3)

            dve.wait_ge(norm_parts, 5)
            for g in range(2):
                then(nc.vector.tensor_reduce(kmean[:, g:g + 1], parts[:, 2 * g + 1, 0, :], AX, ALU.add))
                nc.vector.tensor_scalar(sel16[:, 1 + g, :], sel[:], kmean[:, g:g + 1], 1.0 / S, ALU.mult, ALU.mult).then_inc(kmean_ready, 1)
            dve.wait_ge(norms_ps, 1)
            q_norm = ps[:, 7, 0:NT * H].rearrange("p (t h) -> p t h", t=NT)
            k_norm = ps[:, 7, NT * H:2 * NT * H].rearrange("p (t h) -> p h t", t=NT)
            mean = ps[:, 6, 0:NT * H].rearrange("p (t h) -> p t h", t=NT)
            then(nc.vector.tensor_scalar(bound[:, 0, :, :], mean, SPAN * SQ8, 0.0, ALU.add, ALU.max))
            then(nc.vector.tensor_scalar(other[:].rearrange("p h t -> p t h"), mean, BELOW * SQ8, None, ALU.add))
            nc.vector.tensor_reduce(knorm[:, 0, :], k_norm, AX, ALU.max).then_inc(kmax_in, 1)
            dve.wait_ge(kmaxT_ps, 1)
            then(nc.vector.tensor_reduce(kdiag[:, 1, 0:1], ps[0:H, 6, 256:256 + P], AX, ALU.max))
            nc.vector.tensor_scalar(kdiag[:, 0, :], ident[0:H, 0:H], kdiag[:, 1, 0:1], SLACK * SLACK, ALU.mult, ALU.mult).then_inc(kdiag_ready, 1)
            then(nc.vector.tensor_tensor(bound[:, 1, :, :], bound[:, 0, :, :], bound[:, 0, :, :], ALU.mult))
            dve.wait_ge(kmax_ps, 1)
            then(nc.vector.tensor_copy(knorm[:, 1, :], ps[:, 6, 384:384 + H]))
            then(nc.vector.tensor_tensor(bound[:, 2, :, :], q_norm, knorm[:, 1, :].unsqueeze(1).to_broadcast([P, NT, H]), ALU.mult))
            then(nc.vector.tensor_tensor(bound[:, 0, :, :], bound[:, 2, :, :], bound[:, 1, :, :], ALU.is_gt))
            nc.vector.tensor_reduce(use_max[:], bound[:, 0, :, :].rearrange("p t h -> p h t"), AX, ALU.max).then_inc(use_ready, 1)
            dve.wait_ge(use_ps, 1)
            nc.vector.tensor_copy(flags[:], ps[0:1, 6, 400:400 + H]).then_inc(flags_ready, 1)
            def turned_out(n, k):
                dve.wait_ge(hidT_ps, n + 1)
                after(dve, y_ready, n - 1)
                nc.vector.tensor_copy(hidT[:, k % 2, :, :], ps[:, 6 + k % 2, 0:FP].rearrange("p (f s) -> p f s", f=NF)).then_inc(hidT_ready, 1)

            def tile(n, k, last):
                dve.wait_ge(silu_ready, n + 1)
                dve.wait_ge(g_ready, n + 1)
                after(dve, hidT_ps, n - 1)
                nc.vector.tensor_tensor(hid[:, k % 2, 0:F], silu[:, k % 2, :], ps[:, 2 + k % 2, 0:F], ALU.mult).then_inc(hid_ready, 1)
                if not (isinstance(n, int) and n < 1):
                    turned_out(n - 1, k + 1)

            dve.wait_ge(rot_ready, 16)
            nc.vector.memset(hid[:, :, F:FP], 0.0).then_inc(pad_ready, 1)
            run_tiles(dve, tile)
            turned_out(TILES - 1, TILES - 1)

            def tile_max(h, i, between=iter(())):
                for c in range(NC):
                    m = (h * NT + i) * NC + c
                    dve.wait_ge(m_ready, m + 1)
                    nc.vector.tensor_reduce(m4[:, i, c:c + 1], ps[:, M_BANK + c % 2, :], AX, ALU.max).then_inc(m_reduced, 1)
                    next(between, None)

            def half_max(h, half):
                dve.wait_ge(m_reduced, (h * NT + 8 * half + 8) * NC + CREDIT)
                nc.vector.tensor_reduce(mx[:, half, :], m4[:, 8 * half:8 * half + 8, :], AX, ALU.max).then_inc(mx_ready, 1)

            def make_shift(h, half):
                n = h * 2 + half
                dve.wait_ge(mxT_ready, n + 1)
                dve.wait_ge(shift_ld, n * 32)
                nc.vector.tensor_scalar(shift[:, 0, :], ps[0:8, T_BANK, 0:P], -1.0, None, ALU.mult).then_inc(shift_hi, 1)
                yield
                dve.wait_ge(shift_hi, n + 1)
                nc.vector.scalar_tensor_tensor(shift[:, 1, :], ps[0:8, T_BANK, 0:P], -1.0, shift[:, 0, :],
                                               ALU.mult, ALU.subtract).then_inc(shift_ready, 1)
                yield

            def normalise(h, u):
                unit = h * 2 + u
                turned = ps[:, T_BANK, :].rearrange("p (b g d) -> p b g d", b=4, g=4)
                dve.wait_ge(ot_ready, unit + 1 + TURNED)
                dve.wait_ge(attn_ready, unit + TURNED)
                nc.vector.tensor_copy(half_sum[:], turned[:, :, 2:4, 0:D + 1]).then_inc(half_ready, 1)
                yield
                dve.wait_ge(half_ready, unit + 1)
                nc.vector.tensor_tensor(sums[:], turned[:, :, 0:2, 0:D + 1], half_sum[:], ALU.add).then_inc(sum_ready, 1)
                yield
                dve.wait_ge(sum_ready, unit + 1 + TURNED)
                nc.vector.reciprocal(rden[:], sums[:, :, :, D:D + 1]).then_inc(rden_ready, 1)
                yield
                dve.wait_ge(rden_ready, unit + 1)
                nc.vector.tensor_tensor(attn[:, 8 * u:8 * u + 8, bass.ds(h * D, D)].rearrange("p (c b) d -> p b c d", c=2),
                                        sums[:, :, :, 0:D], rden[:].to_broadcast([P, 4, 2, D]), ALU.mult).then_inc(attn_ready, 1)
                yield

            def no_max(h, i0, n):
                if not (isinstance(h, int) and h == 0):
                    dve.wait_ge(mx_ready, h * 2)
                nc.vector.tensor_copy(m4[:, i0:i0 + n, :], other[:, bass.ds(h, 1), i0:i0 + n].rearrange("p o t -> p (o t)")
                                      .unsqueeze(2).to_broadcast([P, n, NC])).then_inc(m_reduced, n * NC)

            dve.wait_ge(flags_ready, 1)
            need = dve.value_load(flags[0:1, 0:1], min_val=0, max_val=P)
            with dve.If(need != 0):
                for i in range(LEAD):
                    tile_max(0, i)
            with dve.Else():
                no_max(0, 0, LEAD)
            half_max(0, 0)
            for _ in make_shift(0, 0):
                pass

            def step(h, par, s, first, last, with_max):
                beside = iter(())
                if s == 3 and not first:
                    beside = normalise(h - 1, 1)
                if s == 11:
                    beside = normalise(h, 0)
                if s == 6:
                    beside = make_shift(h, 1)
                if s == 14 and not last:
                    beside = make_shift(h + 1, 0)
                if with_max and s < 4:
                    tile_max(h, s + LEAD, beside)
                elif with_max:
                    tile_max(h + 1, s - 4, beside)
                for _ in beside:
                    pass
                if s == 3:
                    half_max(h, 1)
                if s == 11 and not last:
                    half_max(h + 1, 0)

            def add_result(j):
                r, t = j // NT, j % NT
                dve.wait_ge(gather_ld, 2 * NT * 16)
                if r == 1:
                    dve.wait_ge(y_added, t + 1)
                nc.vector.scalar_tensor_tensor(acc[:, t, :], gathered[:, r, t, :], top[:, 6 + r, t:t + 1], acc[:, t, :],
                                               ALU.mult, ALU.add).then_inc(y_added, 1)

            flag = [need]

            def run(part, steps, first, last):
                h = steps[0][0]
                if part == "b" and not last:
                    flag[0] = dve.value_load(flags[0:1, bass.ds(h + 1, 1)], min_val=0, max_val=P)
                if part == "b" and last:
                    for n, (h, par, t) in enumerate(steps):
                        step(h, par, t, first, last, False)
                        for j in range(2 * NT * n // len(steps), 2 * NT * (n + 1) // len(steps)):
                            add_result(j)
                    return
                with dve.If(flag[0] != 0):
                    for h, par, t in steps:
                        step(h, par, t, first, last, True)
                with dve.Else():
                    if part == "a":
                        no_max(h, LEAD, NT - LEAD)
                    else:
                        no_max(h + 1, 0, LEAD)
                    for h, par, t in steps:
                        step(h, par, t, first, last, False)

            run_heads(dve, run)
            for _ in normalise(H - 1, 1):
                pass
            dve.wait_ge(y_added, 2 * NT)
            for q in range(4):
                dve.wait_ge(fin_ps, q + 1)
                nc.vector.tensor_tensor(acc[:, 4 * q:4 * q + 4, :], acc[:, 4 * q:4 * q + 4, :],
                                        ps[:, 4 + q, :].rearrange("p (t d) -> p t d", t=4), ALU.add).then_inc(fin_ready, 1)

        @block.tensor
        def _(pe):
            pe.sem_inc(pv_done, PBUFS)
            pe.sem_inc(ot_ready, TURNED)
            pe.wait_ge(ident_ld, 16)
            pe.wait_ge(const_ld, 3 * 16)
            nc.tensor.transpose(ps[:, 2, 0:3 * E], wqkv_sb[:], ident[0:3 * E, 0:3 * E]).then_inc(wqkv_ps, 1)
            for c in range(NC):
                if c >= 2:
                    pe.wait_ge(xt_ready, c - 1)
                for k in range(4):
                    pe.wait_ge(xn_ready, 4 * c + k + 1)
                    ins = nc.tensor.transpose(ps[:, c % 2, P * k:P * k + P], xn[:, 4 * c + k, :], ident[:])
                ins.then_inc(xt_ps, 1)
            pe.wait_ge(wqkv_ready, 1)
            pe.wait_ge(xt_ready, NC)
            for t in range(NT):
                ins = nc.tensor.matmul(ps[:, 3, 3 * E * t:3 * E * t + 3 * E], xnT[:, P * t:P * t + P], wqkvT[:], start=True, stop=True)
            ins.then_inc(mix_ps, 1)
            pe.wait_ge(wmat_ld, 4 * 16)
            pe.wait_ge(wrap_ready, 1)
            for t in range(NT):
                if t % 4 == 0 and t >= 8:
                    pe.wait_ge(v_ready, t // 4 - 1)
                for ahead in range(2):
                    ins = nc.tensor.matmul(ps[:, 6 + t // 4 % 2, DM * (t % 4):DM * (t % 4) + DM],
                                           xnT[:, P * t + ahead:P * t + ahead + P], wmat[:, 2, :], start=ahead == 0, stop=ahead == 1)
                if t % 4 == 3:
                    ins.then_inc(v_ps, 1)

            def expert_weights(e):
                for b in range(NF):
                    bank = 6 + (e * NF + b) % 2
                    pe.wait_ge(wT_ready, e * NF + b - 1 + CREDIT)
                    for f, (f0, n) in enumerate(FCH):
                        if b < 2:
                            ins = nc.tensor.transpose(ps[:, bank, f0:f0 + n], w1raw[0:n, NF * b + f, e, :], ident[0:n, 0:n])
                        else:
                            ins = nc.tensor.transpose(ps[0:n, bank, DM * f:DM * f + DM], w2raw[:, e, f0:f0 + n], ident[:])
                    ins.then_inc(tr_ready, 1)

            pe.wait_ge(v_ready, 4)
            pe.wait_ge(w_ld, 7 * 16)
            for e in range(E // 2):
                expert_weights(e)
            pe.wait_ge(chosen_ready, 2)
            pe.wait_ge(route_ld, 3 * 16)
            pe.wait_ge(ones_ready, ONES)
            nc.tensor.matmul(ps[:, 3, 0:(NT + 1) * E], tri[:], chosen[:].rearrange("p t e -> p (t e)"), start=True, stop=False)
            for t in range(NT):
                ins = nc.tensor.matmul(ps[:, 3, E * (t + 1):E * (NT + 1)], ones[:], chosen[:, t:t + 1, :].to_broadcast([P, NT - t, E]),
                                       start=False, stop=t == NT - 1)
            ins.then_inc(rank_ps, 1)
            for e in range(E // 2, E):
                expert_weights(e)
            for n in range(16):
                i, c = n // NC, n % NC
                g, which = i // 2, i % 2
                if n >= 2:
                    pe.wait_ge(rot_ready, n - 1)
                for half in range(2):
                    ins = nc.tensor.matmul(ps[64 * half:64 * half + 64, 4 + n % 2, :], wmat[:, which, 64 * g:64 * g + 64],
                                           xnT[:, CW * c:CW * c + CW], start=True, stop=True, tile_position=(0, 64 * half))
                ins.then_inc(proj_ps, 1)

            pe.wait_ge(wT_ready, E * NF + CREDIT)
            pe.wait_ge(norm_parts, 5)
            pe.wait_ge(kmean_ready, 2)
            for t in range(NT):
                for i in range(4):
                    at = (i % 2) * NT * H + t * H + (i // 2) * 8
                    nc.tensor.matmul(ps[:, 7, at:at + 8], squares[i][:, P * t:P * t + P], sel16[:, 0, :], start=True, stop=True)
                for g in range(2):
                    at = t * H + g * 8
                    ins = nc.tensor.matmul(ps[:, 6, at:at + 8], parts[:, 2 * g, 0, P * t:P * t + P], sel16[:, 1 + g, :], start=True, stop=True)
            ins.then_inc(norms_ps, 1)
            pe.wait_ge(kmax_in, 1)
            nc.tensor.transpose(ps[0:H, 6, 256:256 + P], knorm[:, 0, :], ident[:]).then_inc(kmaxT_ps, 1)
            pe.wait_ge(kdiag_ready, 1)
            nc.tensor.matmul(ps[:, 6, 384:384 + H], ones[0:H, :], kdiag[:, 0, :], start=True, stop=True).then_inc(kmax_ps, 1)
            pe.wait_ge(use_ready, 1)
            nc.tensor.matmul(ps[0:1, 6, 400:400 + H], ones[:, 0:1], use_max[:], start=True, stop=True).then_inc(use_ps, 1)
            pe.wait_ge(flags_ready, 1)

            def turn_rows(n, k):
                pe.wait_ge(xg_ld[k // 2 % 2], (n - k % 4) * 4 + 16)
                after(pe, xgT_ready, n)
                nc.tensor.transpose(ps[:, 4, 0:P], xg[:, k % 4, :], ident[:]).then_inc(xgT_ps, 1)

            def turn_hidden(n, k):
                pe.wait_ge(hid_ready, n + 1)
                after(pe, hidT_ready, n - 1)
                for f in range(NF):
                    ins = nc.tensor.transpose(ps[:, 6 + k % 2, P * f:P * f + P], hid[:, k % 2, P * f:P * f + P], ident[:])
                ins.then_inc(hidT_ps, 1)

            def expert_of_tile(n):
                return pe.value_load(expert_of[0:1, bass.ds(n, 1)], min_val=0, max_val=E - 1)

            def result(n, k):
                e = expert_of_tile(n)
                pe.wait_ge(hidT_ready, n + 1)
                after(pe, y_copied, n)
                for f, (f0, rows) in enumerate(FCH):
                    ins = nc.tensor.matmul(ps[:, 5, 0:DM], hidT[0:rows, k % 2, f, :],
                                           w2T[0:rows, bass.ds(e, 1), f, :].rearrange("p o h -> p (o h)"), start=f == 0, stop=f == NF - 1)
                ins.then_inc(y_ready, 1)

            def tile(n, k, last):
                e = expert_of_tile(n)
                pe.wait_ge(xgT_ready, n + 1)
                after(pe, silu_ready, n - 1)
                nc.tensor.matmul(ps[:, k % 2, 0:F], xgT[:, k % 2, :], w1T[:, bass.ds(e, 1), 0:F].rearrange("p o f -> p (o f)"),
                                 start=True, stop=True).then_inc(a_ready, 1)
                if not last:
                    turn_rows(n + 1, k + 1)
                after(pe, hid_ready, n - 1)
                nc.tensor.matmul(ps[:, 2 + k % 2, 0:F], xgT[:, k % 2, :], w1T[:, bass.ds(e, 1), F:2 * F].rearrange("p o f -> p (o f)"),
                                 start=True, stop=True).then_inc(g_ready, 1)
                if not (isinstance(n, int) and n < 1):
                    turn_hidden(n - 1, k + 1)
                if not (isinstance(n, int) and n < 2):
                    result(n - 2, k + 2)

            pe.wait_ge(rot_ready, 16)
            pe.wait_ge(owner_ready, 1)
            pe.wait_ge(pad_ready, 1)
            turn_rows(0, 0)
            run_tiles(pe, tile)
            turn_hidden(TILES - 1, TILES - 1)
            for n in range(TILES - 2, TILES):
                result(n, n)
            pe.wait_ge(silu_ready, TILES)
            pe.wait_ge(hid_ready, TILES)
            pe.wait_ge(hidT_ready, TILES)
            pe.wait_ge(y_copied, TILES)

            def scores(h, par, s, skipped):
                g = h * STEPS + s
                u, k = s // 8, s % 8
                if k == 0:
                    pe.wait_ge(shift_ld, (h * 2 + u + 1) * 32)
                for b in range(2):
                    t = 2 * k + b
                    pe.wait_ge(exp_done, g * 2 + b - 1 + CREDIT)
                    for c in range(2):
                        col = CW * (2 * u + c)
                        ins = nc.tensor.matmul(ps[:, SCORE_BANKS + 2 * b + c, :], ka[par][:, P * t:P * t + P],
                                               qa[par][:, col:col + CW], start=True, stop=True)
                        if skipped and b == 0 and c == 0:
                            ins.then_inc(m_ready, skipped)
                    ins.then_inc(score_ready, 1)
                    yield

            def max_scores(h, par, i):
                for c in range(NC):
                    m = (h * NT + i) * NC + c
                    pe.wait_ge(m_reduced, m - 1 + CREDIT)
                    nc.tensor.matmul(ps[:, M_BANK + c % 2, :], qa[par][0:KQ, P * i:P * i + P],
                                     ka[par][0:KQ, CW * c:CW * c + CW], start=True, stop=True).then_inc(m_ready, 1)
                    yield

            def weighted_values(h, par, s):
                g = h * STEPS + s
                u, k = s // 8, s % 8
                if s == 0:
                    pe.wait_ge(vh_ready, h + 1)
                if k == 0:
                    pe.wait_ge(o_copied, h * 2 + u)
                pe.wait_ge(exp_done, g * 2 + 2 + CREDIT)
                for b in range(2):
                    for c in range(2):
                        col = 32 * (2 * b + c)
                        ins = nc.tensor.matmul(ps[col:col + 32, O_BANK, :], vh[:, par, 2 * k + b, :], probs[:, s % PBUFS, b, c, :],
                                               start=k == 0, stop=k == 7, tile_position=(0, col))
                ins.then_inc(pv_done, 1)

            def turn_max(h, half):
                pe.wait_ge(mx_ready, h * 2 + half + 1)
                if not (isinstance(h, int) and h == 0 and half == 0):
                    pe.wait_ge(sum_ready, h * 2 + half - 1 + TURNED)
                nc.tensor.transpose(ps[0:8, T_BANK, 0:P], mx[:, half, :], ident[:]).then_inc(mxT_ready, 1)

            def turn_out(h, u):
                unit = h * 2 + u
                pe.wait_ge(o_copied, unit + 1)
                pe.wait_ge(shift_ready, unit + 1)
                pe.wait_ge(sum_ready, unit + TURNED)
                for b in range(4):
                    ins = nc.tensor.transpose(ps[:, T_BANK, P * b:P * b + P], osb[:, P * b:P * b + P], ident[:])
                ins.then_inc(ot_ready, 1)

            def all_of(gen):
                for _ in gen:
                    pass

            pe.wait_ge(aug_ld, 12 * 16)
            need = pe.value_load(flags[0:1, 0:1], min_val=0, max_val=P)
            with pe.If(need != 0):
                for i in range(LEAD):
                    all_of(max_scores(0, 0, i))
            with pe.Else():
                pe.sem_inc(m_ready, LEAD * NC)
            turn_max(0, 0)

            def step(h, par, s, first, last, with_max, skipped=0):
                if s == 4 and not last:
                    pe.wait_ge(aug_ld, h * 192 + 384)
                sc = scores(h, par, s, skipped)
                ms = iter(())
                if with_max:
                    ms = max_scores(h, par, s + LEAD) if s < 4 else max_scores(h + 1, 1 - par, s - 4)
                all_of(sc)
                next(ms, None)
                next(ms, None)
                if s >= PV_LAG:
                    weighted_values(h, par, s - PV_LAG)
                elif not first:
                    weighted_values(h - 1, 1 - par, s - PV_LAG + STEPS)
                all_of(ms)
                if s == 2 and not first:
                    turn_out(h - 1, 1)
                if s == 10:
                    turn_out(h, 0)
                if s == 5:
                    turn_max(h, 1)
                if s == 13 and not last:
                    turn_max(h + 1, 0)

            flag = [need]

            def run(part, steps, first, last):
                h = steps[0][0]
                if part == "b" and not last:
                    flag[0] = pe.value_load(flags[0:1, bass.ds(h + 1, 1)], min_val=0, max_val=P)
                if part == "b" and last:
                    for h, par, t in steps:
                        step(h, par, t, first, last, False)
                    return
                with pe.If(flag[0] != 0):
                    for h, par, t in steps:
                        step(h, par, t, first, last, True)
                with pe.Else():
                    for n, (h, par, t) in enumerate(steps):
                        step(h, par, t, first, last, False, len(steps) * NC if n == 0 else 0)

            run_heads(pe, run)
            for s in range(STEPS - PV_LAG, STEPS):
                weighted_values(H - 1, 1, s)
            turn_out(H - 1, 1)
            pe.wait_ge(attn_ready, 2 * H + TURNED)
            pe.wait_ge(wo_ready, 1)
            for q in range(4):
                for k in range(4):
                    ins = nc.tensor.transpose(ps[:, q, P * k:P * k + P], attn[:, 4 * q + k, :], ident[:])
                ins.then_inc(at_ps, 1)
            for q in range(4):
                pe.wait_ge(at_ready, q + 1)
                for k in range(4):
                    t = 4 * q + k
                    ins = nc.tensor.matmul(ps[:, 4 + q, DM * k:DM * k + DM], attnT[:, P * t:P * t + P], wo_mod[:], start=True, stop=True)
                ins.then_inc(fin_ps, 1)


_INS = ["L0_attn_x", "L0_attn_Wq", "L0_attn_Wk", "L0_attn_Wv", "L0_attn_Wo", "L0_attn_quantum_phase",
        "L0_attn_quantum_amplitude", "L0_ffn_wqkv", "L0_ffn_w1", "L0_ffn_w2"]


def kernel(**inputs):
    import concourse.bacc as _bacc
    from concourse.bass_utils import run_bass_kernel_spmd as _run

    angle = 2.0 * np.pi * np.arange(S, dtype=np.float64) / S
    rows = np.stack([np.cos(angle), np.sin(angle)]).astype(np.float32)
    shape_constants = {
        "identity": np.eye(P, dtype=np.float32),
        "descending": np.tile(np.arange(E, 0, -1, dtype=np.float32), (P, 1)),
        "cos_sin": np.repeat(rows, P // 2, axis=0),
        "head_of_row": np.tile(np.repeat(np.eye(8, dtype=np.float32), D, axis=0), (2, 1)),
        "earlier": np.triu(np.ones((P, P), np.float32), 1),
        "lower_expert": np.tile(np.tril(np.ones((E, E), np.float32), -1), (P, 1, 1)),
        "tile_number": np.repeat(np.arange(TILES, dtype=np.float32), E).reshape(1, TILES, E),
    }
    nc = _bacc.Bacc("TRN2", target_bir_lowering=False, num_devices=1)
    arrays, args = {}, []
    for name in _INS:
        arrays[f"in_{name}"] = np.ascontiguousarray(inputs[name])
    arrays.update(shape_constants)
    for name, a in arrays.items():
        args.append(nc.dram_tensor(name, a.shape, mybir.dt.from_np(a.dtype), kind="ExternalInput").ap())
    out = nc.dram_tensor("out", (1, S, DM), F32, kind="ExternalOutput").ap()
    build(nc, *args, out)
    result = _run(nc, [arrays], core_ids=[0])
    return result.results[0]["out"]
```
